# Optimizing a Trainium2 kernel written in Bass

```python
import numpy as np
import jax
import jax.numpy as jnp

def _softmax(x, axis=-1):
    return jax.nn.softmax(x, axis=axis)

def _gelu(x):
    return jax.nn.gelu(x, approximate=True)

def _silu(x):
    return jax.nn.silu(x)

def _sigmoid(x):
    return jax.nn.sigmoid(x)

def _layernorm(x, axis=-1, eps=1e-05):
    m = jnp.mean(x, axis=axis, keepdims=True)
    v = jnp.var(x, axis=axis, keepdims=True)
    return (x - m) / jnp.sqrt(v + eps)

def _scatter_add(tgt, idx, src, axis=0):
    return tgt.at[idx].add(src)

def _segment_sum(src, seg, n):
    return jax.ops.segment_sum(src, seg, n)
kernel_name = 'mk_flamingo_gated_d1_seqx_r4_e060ec'

def setup_inputs(seed: int=0):
    np.random.seed(seed)
    _w = jnp.asarray

    def _rec_inputs():
        import jax
        import jax.numpy as jnp
        _rk = jax.random.key(seed)
        x = 7.22e-05 + 1 * jax.random.normal(jax.random.fold_in(_rk, 1), (32, 128, 512), jnp.float32)
        _lenS = 128 - jax.random.randint(jax.random.fold_in(_rk, 7), (32,), 0, max(1, 128 // 4) + 1, jnp.int32)
        _lenS2 = 128 - jax.random.randint(jax.random.fold_in(_rk, 8), (32,), 0, max(1, 128 // 4) + 1, jnp.int32)
        _ctx_512P = jax.random.normal(jax.random.fold_in(_rk, 11), (32, 16, 128), jnp.float32)
        _ctx_512c = jax.random.dirichlet(jax.random.fold_in(_rk, 511), 0.3 * jnp.ones((16,), jnp.float32), (32, 128))
        _ctx_512t = jnp.einsum('bsk,bkd->bsd', _ctx_512c, _ctx_512P)
        _ctx_512t = _ctx_512t * jax.lax.rsqrt(jnp.mean(jnp.square(_ctx_512t)) + 1e-12) * 0.953939
        ctx_512 = -0.000514642 + 1.00011 * (_ctx_512t + 0.3 * jax.random.normal(jax.random.fold_in(_rk, 611), (32, 128, 128), jnp.float32))
        _g = jax.random.normal(jax.random.fold_in(_rk, 9001), (2, 1), jnp.float32)
        _g = jnp.sign(_g) * jnp.maximum(jnp.abs(_g), 1.0) + (_g == 0) * 1.0
        g_xattn = _g[0]
        g_ffn = _g[1]
        return (x, ctx_512, g_xattn, g_ffn)
    x, ctx_512, g_xattn, g_ffn = _rec_inputs()

    def _L0_xattn_setup():
        import jax, jax.numpy as jnp
        import numpy as np
        import math
        NUM_Q_HEADS = 32
        NUM_KV_HEADS = 8
        key = jax.random.key(seed)
        k1, k2, k3 = jax.random.split(key, 3)
        B, S, E = (2, 512, 512)
        kv_E = NUM_KV_HEADS * (E // NUM_Q_HEADS)
        q = jax.random.normal(k1, (B, S, E), dtype=jnp.float32)
        k = jax.random.normal(k2, (B, S, kv_E), dtype=jnp.float32)
        v = jax.random.normal(k3, (B, S, kv_E), dtype=jnp.float32)
        return {'q': q, 'k': k, 'v': v}
    _L0_xattn_all = _L0_xattn_setup()
    _L0_xattn_in = {k: v for k, v in _L0_xattn_all.items() if k in ()}
    del _L0_xattn_all

    def _L0_ffn_setup():
        import jax, jax.numpy as jnp
        import numpy as np
        D = 512
        H_TOTAL = 2048
        E = 8
        K = 2
        HE = H_TOTAL // E
        B, S = (2, 512)
        key = jax.random.key(seed)
        ks = jax.random.split(key, 8)
        scale_up = 1.0 / np.sqrt(D)
        scale_dn = 1.0 / np.sqrt(HE)
        return {'x': jax.random.normal(ks[0], (B, S, D), dtype=jnp.float32), 'Wg1': jax.random.normal(ks[1], (E, D), dtype=jnp.float32) * 0.02, 'Wg2': jax.random.normal(ks[2], (E, E), dtype=jnp.float32) * 0.2, 'Wup': jax.random.uniform(ks[3], (E, HE, D), dtype=jnp.float32, minval=-scale_up, maxval=scale_up), 'bup': jax.random.uniform(ks[4], (E, HE), dtype=jnp.float32, minval=-scale_up, maxval=scale_up), 'Wdown': jax.random.uniform(ks[5], (E, D, HE), dtype=jnp.float32, minval=-scale_dn, maxval=scale_dn), 'bdown': jax.random.uniform(ks[6], (E, D), dtype=jnp.float32, minval=-scale_dn, maxval=scale_dn)}
    _L0_ffn_all = _L0_ffn_setup()
    _L0_ffn_in = {k: v for k, v in _L0_ffn_all.items() if k in ('Wg1', 'Wg2', 'Wup', 'bup', 'Wdown', 'bdown')}
    del _L0_ffn_all
    return {'x': x, 'ctx_512': ctx_512, 'g_xattn': g_xattn, 'g_ffn': g_ffn, 'L0_ffn_Wg1': _L0_ffn_in['Wg1'], 'L0_ffn_Wg2': _L0_ffn_in['Wg2'], 'L0_ffn_Wup': _L0_ffn_in['Wup'], 'L0_ffn_bup': _L0_ffn_in['bup'], 'L0_ffn_Wdown': _L0_ffn_in['Wdown'], 'L0_ffn_bdown': _L0_ffn_in['bdown']}

def reference(x, ctx_512, g_xattn, g_ffn, L0_ffn_Wg1, L0_ffn_Wg2, L0_ffn_Wup, L0_ffn_bup, L0_ffn_Wdown, L0_ffn_bdown):
    import jax
    import jax.numpy as jnp

    def _L0_xattn_ref(q, k, v):
        import jax, jax.numpy as jnp
        import numpy as np
        import math
        NUM_Q_HEADS = 32
        NUM_KV_HEADS = 8
        B, S, E = q.shape
        H, KV = (NUM_Q_HEADS, NUM_KV_HEADS)
        D = E // H
        G = H // KV
        scale = math.sqrt(D)
        qh = q.reshape(B, S, KV, G, D).transpose(0, 2, 3, 1, 4)
        kh = k.reshape(B, S, KV, D).transpose(0, 2, 1, 3)
        vh = v.reshape(B, S, KV, D).transpose(0, 2, 1, 3)
        scores = jnp.einsum('bkgsd,bktd->bkgst', qh, kh) / scale
        weights = jax.nn.softmax(scores, axis=-1)
        out = jnp.einsum('bkgst,bktd->bkgsd', weights, vh)
        return out.transpose(0, 3, 1, 2, 4).reshape(B, S, E)

    def _L0_ffn_ref(x, Wg1, Wg2, Wup, bup, Wdown, bdown):
        import jax, jax.numpy as jnp
        import numpy as np
        D = 512
        H_TOTAL = 2048
        E = 8
        K = 2
        HE = H_TOTAL // E
        B, S = (2, 512)
        Bd, Sd, Dd = x.shape
        T = Bd * Sd
        xt = x.reshape(T, Dd)
        logits = jnp.tanh(xt @ Wg1.T) @ Wg2.T
        _, top_idx = jax.lax.top_k(logits, K)
        top_logits = jnp.take_along_axis(logits, top_idx, axis=1)
        top_scores = jax.nn.softmax(top_logits.astype(jnp.float32), axis=1).astype(logits.dtype)
        rows = jnp.arange(T)[:, None]
        scores = jnp.zeros_like(logits).at[rows, top_idx].set(top_scores)
        up = jnp.einsum('td,ehd->teh', xt, Wup) + bup
        h = jax.nn.silu(up)
        down = jnp.einsum('teh,eoh->teo', h, Wdown) + bdown
        out = jnp.einsum('te,teo->to', scores, down)
        return out.reshape(Bd, Sd, Dd)
    x = x + jnp.tanh(g_xattn[0]) * _L0_xattn_ref(_layernorm(x, axis=-1), ctx_512, ctx_512)
    x = x + jnp.tanh(g_ffn[0]) * _L0_ffn_ref(_layernorm(x, axis=-1), L0_ffn_Wg1, L0_ffn_Wg2, L0_ffn_Wup, L0_ffn_bup, L0_ffn_Wdown, L0_ffn_bdown)
    return x

_drawn_inputs = setup_inputs


def setup_inputs(seed=0):
    import zlib

    import numpy as np

    out = dict(_drawn_inputs(seed))
    spreads = {}
    factors = {'L0_ffn_bup': 8.0, 'L0_ffn_bdown': 2.874}
    for name, (base, spread) in spreads.items():
        noise = np.random.default_rng([zlib.crc32(name.encode()), seed]).standard_normal(out[name].shape)
        drawn = base * np.exp(spread * noise) if base else spread * noise
        out[name] = jnp.asarray(drawn.astype(out[name].dtype))
    for name, factor in factors.items():
        out[name] = (out[name] * factor).astype(out[name].dtype)
    return out
```

```python
import concourse.bass as bass
from concourse import mybir
from contextlib import ExitStack

F32 = mybir.dt.float32
F32R = mybir.dt.float32r
BF16 = mybir.dt.bfloat16
I32 = mybir.dt.int32
U32 = mybir.dt.uint32
ALU = mybir.AluOpType
ACT = mybir.ActivationFunctionType
X_AXIS = mybir.AxisListType.X

P = 128
B, S, D = 32, 128, 512
KV, G, HD = 8, 4, 16
H = KV * G
E, HE = 8, 256
DC, HC = D // P, HE // P
PARTS = 6
QROWS = PARTS * HD
MROWS = 3
MHALF = KV // 2 * (G + 1)
MWIDE = 68
KQ = P + G * P
REGION = B * S + P
TILES = 2 * B * S // P + E - 1
DUMMY = E - 1
ROWS = E * REGION + DUMMY * P
WCHUNK = 512
WCOLS = E * (DC * HE + HC * D)
DOWN0 = E * DC * HE
EPS = 1e-5
O_LOAD, O_NORM, O_QT, O_S, O_ST, O_OUT, O_GATE, O_ROUTE, O_SLOT = range(9)
STEPS = B + O_SLOT
LOOP0 = 12
RING = 4


def valid(b, n=B):
    return not isinstance(b, int) or 0 <= b < n


def wait(eng, sem, value):
    if not isinstance(value, int) or value > 0:
        eng.wait_ge(sem, value)


def pipeline(eng, step, steps, first, last, unroll):
    for s in range(first):
        step(s, s % unroll)
    with eng.Fori(0, (last - first) // unroll) as i:
        for u in range(unroll):
            step(i * unroll + (first + u), (first + u) % unroll)
    for s in range(last, steps):
        step(s, s % unroll)


def block_kernel(nc, x_d, ctx_d, gx_d, gf_d, wg1_d, wg2_d, w_d, bup_d, bdn_d, out_d):
    slots_d = nc.dram_tensor("slots", (ROWS, D), F32, kind="Internal").ap()
    y_d = nc.dram_tensor("expert_out", (TILES * P, D), F32, kind="Internal").ap()
    x2_d = nc.dram_tensor("x2_scratch", (B, S, D), F32, kind="Internal").ap()

    top = ExitStack()
    with top:
        def sb(name, shape, dt, stack=top):
            return stack.enter_context(nc.sbuf_tensor(name, shape, dt))

        def sem(name):
            return top.enter_context(nc.semaphore(name))

        w_hi = sb("w_hi", [P, WCOLS], F32R)
        w_lo = sb("w_lo", [P, WCOLS], F32R)
        slot_all = sb("slot_all", [P, 2 * B], F32)
        rows_all = sb("rows_all", [P, 2 * B], I32)
        gap_all = sb("gap_all", [P, B], F32)
        run = sb("run", [P, E], F32)
        ebase = sb("ebase", [P, E], F32)
        tick = sb("tick", [P, 1], F32)
        tock = sb("tock", [P, 3], F32)
        iota_p = sb("iota_p", [P, 1], F32)
        ident_f = sb("ident_f", [P, P], F32)
        gates = sb("gates", [P, 2], F32)
        gates_raw = sb("gates_raw", [P, 2], F32)

        p1 = ExitStack()
        wst = sb("wst", [P, WCHUNK], F32, p1)
        x_in = [sb(f"x_in{i}", [P, D], F32, p1) for i in range(2)]
        c_in = [sb(f"c_in{i}", [P, P], F32, p1) for i in range(2)]
        q_nat = [sb(f"q_nat{i}", [P, H * 4 * HD], BF16, p1) for i in range(2)]
        k_nat = [sb(f"k_nat{i}", [P, KV * QROWS], BF16, p1) for i in range(2)]
        k_rem = sb("k_rem", [P, P], F32, p1)
        v_aug = [sb(f"v_aug{i}", [P, KV * 32], F32, p1) for i in range(RING)]
        kq = [sb(f"kq{i}", [P, KV * KQ], BF16, p1) for i in range(2)]
        probs = sb("probs", [P, KV * G * S], F32, p1)
        o_sb = sb("o_sb", [P, G * S], F32, p1)
        x_res = [sb(f"x_res{i}", [P, D], F32, p1) for i in range(2)]
        z = [sb(f"z{i}", [P, D], F32, p1) for i in range(RING)]
        z_t = sb("z_t", [P, D], F32, p1)
        nmax = [sb(f"nmax{i}", [P, H], F32, p1) for i in range(2)]
        nm_rem = [sb(f"nm_rem{i}", [P, H // 2], F32, p1) for i in range(2)]
        nm_parts = [sb(f"nm_parts{i}", [P, MWIDE], BF16, p1) for i in range(2)]
        mt_sb = [sb(f"mt_sb{i}", [MROWS * MHALF, S], BF16, p1) for i in range(2)]
        ident_b = sb("ident_b", [P, P], BF16, p1)
        before = sb("before", [P, P], BF16, p1)
        ones_b = sb("ones_b", [P, P], BF16, p1)
        iota_e = sb("iota_e", [P, E], F32, p1)
        wg1 = sb("wg1", [P, DC * E], F32, p1)
        wg2 = sb("wg2", [E, E], F32, p1)
        st_n = sb("st_n", [P, 6], F32, p1)
        mv_n = sb("mv_n", [P, 2], F32, p1)
        ve_n = sb("ve_n", [P, 1], F32, p1)
        rs_n = sb("rs_n", [P, 1], F32, p1)
        st_o = sb("st_o", [P, 6], F32, p1)
        mv_o = sb("mv_o", [P, 2], F32, p1)
        ve_o = sb("ve_o", [P, 1], F32, p1)
        rs_o = sb("rs_o", [P, 1], F32, p1)
        minus_half = sb("minus_half", [P, 1], F32, p1)
        eps = sb("eps", [P, 1], F32, p1)
        rden = sb("rden", [P, G * 4], F32, p1)
        rgate = sb("rgate", [P, G * 4], F32, p1)
        th_sb = sb("th_sb", [E, S], F32, p1)
        lg_sb = [sb(f"lg_sb{i}", [P, E], F32, p1) for i in range(2)]
        top8 = sb("top8", [P, E], F32, p1)
        idx8 = sb("idx8", [P, E], U32, p1)
        idxf = sb("idxf", [P, 2], F32, p1)
        m1 = [sb(f"m1_{i}", [P, E], F32, p1) for i in range(2)]
        m2 = [sb(f"m2_{i}", [P, E], F32, p1) for i in range(2)]
        m12 = [sb(f"m12_{i}", [P, E], BF16, p1) for i in range(2)]
        pos = sb("pos", [P, E], F32, p1)
        junk = sb("junk", [P, 3 * E], F32, p1)
        slot_f = sb("slot_f", [P, 2], F32, p1)
        slot_i = [sb(f"slot_i{i}", [P, 2], I32, p1) for i in range(RING)]
        p1.close()

        p2 = ExitStack()
        bup = sb("bup", [P, E * HE], F32, p2)
        bdn = sb("bdn", [P, E * D], F32, p2)
        z_s = [sb(f"z_s{i}", [P, D], F32, p2) for i in range(2)]
        zh = [sb(f"zh{i}", [P, D], F32R, p2) for i in range(2)]
        zl = [sb(f"zl{i}", [P, D], F32R, p2) for i in range(2)]
        u_sb = [sb(f"u_sb{i}", [P, HE], F32, p2) for i in range(2)]
        t_sb = [sb(f"t_sb{i}", [P, HE], F32, p2) for i in range(2)]
        h_sb = [sb(f"h_sb{i}", [P, HE], F32, p2) for i in range(2)]
        hh = [sb(f"hh{i}", [P, HE], F32R, p2) for i in range(2)]
        hl = [sb(f"hl{i}", [P, HE], F32R, p2) for i in range(2)]
        y_sb = [sb(f"y_sb{i}", [P, D], F32, p2) for i in range(2)]
        zeros = sb("zeros", [P, D], F32, p2)
        count = sb("count", [P, E], F32, p2)
        i128 = sb("i128", [P, B], F32, p2)
        over = sb("over", [P, E * B], F32, p2)
        ntile = sb("ntile", [P, E], F32, p2)
        tend = sb("tend", [P, E], F32, p2)
        tskip = sb("tskip", [P, E], F32, p2)
        iota_t = sb("iota_t", [P, TILES], F32, p2)
        past = sb("past", [P, TILES * E], F32, p2)
        pastw = sb("pastw", [P, TILES * E], F32, p2)
        tile_e = sb("tile_e", [P, TILES], F32, p2)
        tile_r = sb("tile_r", [P, TILES], F32, p2)
        tab_e = sb("tab_e", [P, TILES], I32, p2)
        tab_r = sb("tab_r", [P, TILES], I32, p2)
        pad_f = sb("pad_f", [P, E], F32, p2)
        pad_i = sb("pad_i", [P, E], I32, p2)
        beyond = sb("beyond", [P, 2 * B * E], F32, p2)
        drop = sb("drop", [P, E], F32, p2)
        shift = sb("shift", [P, 2 * B], F32, p2)
        egap = sb("egap", [P, B], F32, p2)
        sden = sb("sden", [P, B], F32, p2)
        coef = [sb(f"coef{i}", [P, B], F32, p2) for i in range(2)]
        p2.close()

        bank = [top.enter_context(nc.psum_tensor(f"bank{i}", [P, 512], F32)) for i in range(8)]
        s_ps, st_ps, qt_ps, bank_a, bank_b = bank[0:2], bank[2:4], bank[4:6], bank[6], bank[7]

        const_ready = sem("const_ready")
        const_dma = sem("const_dma")
        gate_ready = sem("gate_ready")
        x_loaded = [sem(f"x_loaded{i}") for i in range(2)]
        c_loaded = [sem(f"c_loaded{i}") for i in range(2)]
        res_loaded = [sem(f"res_loaded{i}") for i in range(2)]
        w_loaded = sem("w_loaded")
        w_hi_done, w_lo_done = sem("w_hi_done"), sem("w_lo_done")
        n_stats, n_mv, n_ve, n_rs, n_done = (sem(f"n_{n}") for n in ("stats", "mv", "ve", "rs", "done"))
        q_hi, q_rem, q_mid, q_lo = (sem(f"q_{n}") for n in ("hi", "rem", "mid", "lo"))
        k_hi, k_rem_done, k_mid, k_lo, v_done = (sem(n) for n in ("k_hi", "k_rem_done", "k_mid", "k_lo", "v_done"))
        qt_done, qt_act, qt_dve = sem("qt_done"), sem("qt_act"), sem("qt_dve")
        s_done, max_done = sem("s_done"), sem("max_done")
        nm_hi, nm_remd, nm_mid, nm_lo = (sem(f"nm_{n}") for n in ("hi", "remd", "mid", "lo"))
        mt_done, mt_copied = sem("mt_done"), sem("mt_copied")
        mrow = [sem(f"mrow{i}") for i in range(2)]
        st_done, exp_done, pv_done, o_copied, on_done = (
            sem(n) for n in ("st_done", "exp_done", "pv_done", "o_copied", "on_done"))
        rden_done, rgate_done, att_done, res_done = (sem(n) for n in ("rden_done", "rgate_done", "att_done", "res_done"))
        res_stored = [sem(f"res_stored{i}") for i in range(2)]
        o_stats, o_mv, o_ve, o_rs, z_done = (sem(n) for n in ("o_stats", "o_mv", "o_ve", "o_rs", "z_done"))
        zt_done, zt_copied, lg1_done, th_done, lg2_done, lg_copied = (
            sem(n) for n in ("zt_done", "zt_copied", "lg1_done", "th_done", "lg2_done", "lg_copied"))
        top_done, idx_done, idxf_done, masks_done, m12_done, gap_done = (
            sem(n) for n in ("top_done", "idx_done", "idxf_done", "masks_done", "m12_done", "gap_done"))
        rank_done, pos_done, run_done, slot_done, sloti_done, slotall_done = (
            sem(n) for n in ("rank_done", "pos_done", "run_done", "slot_done", "sloti_done", "slotall_done"))
        scattered = [sem(f"scattered{i}") for i in range(RING)]
        phase1_over, phase2_over = sem("phase1_over"), sem("phase2_over")
        bias_loaded, bias_done, dummy_done = sem("bias_loaded"), sem("bias_done"), sem("dummy_done")
        f_const, tab_step, tab_done, pad_idx, pads_done, exp2_done, coef_step = (
            sem(n) for n in ("f_const", "tab_step", "tab_done", "pad_idx", "pads_done", "exp2_done", "coef_step"))
        tile_loaded = [sem(f"tile_loaded{i}") for i in range(2)]
        ft_done, zh_done, zl_done, up_done, u_done, tanh_done, h_done = (
            sem(n) for n in ("ft_done", "zh_done", "zl_done", "up_done", "u_done", "tanh_done", "h_done"))
        ht_done, hh_done, hl_done, dn_done, y_done = (sem(n) for n in ("ht_done", "hh_done", "hl_done", "dn_done", "y_done"))
        y_stored = [sem(f"y_stored{i}") for i in range(2)]
        held = [sem(f"held{i}") for i in range(3)]
        gi_done = sem("gi_done")
        y1_loaded = [sem(f"y1_loaded{i}") for i in range(RING)]
        y2_loaded = [sem(f"y2_loaded{i}") for i in range(RING)]
        r_loaded = [sem(f"r_loaded{i}") for i in range(RING)]
        mix1, mix2 = sem("mix1"), sem("mix2")
        stored = [sem(f"stored{i}") for i in range(RING)]

        p3 = ExitStack()
        keep_coef = sb("over_phase2", [P, 2 * E * D // 4], F32, p3)
        p3.close()
        p3 = ExitStack()
        g_idx = [sb(f"g_idx{i}", [P, 2], I32, p3) for i in range(RING)]
        y1 = [sb(f"y1_{i}", [P, D], F32, p3) for i in range(RING)]
        y2 = [sb(f"y2_{i}", [P, D], F32, p3) for i in range(RING)]
        r_in = [sb(f"r_in{i}", [P, D], F32, p3) for i in range(RING)]
        p3.close()

        block = top.enter_context(nc.Block())

        def ring2(b, p, per=16):
            return (b - p) * (per // 2) + per

        def ring4(b, q, per):
            return (b - q) * (per // 4) + per

        @block.sync
        def _(sp):
            sp.dma_start(gates_raw[:, 0:1], gx_d.rearrange("(a n) -> a n", a=1).to_broadcast([P, 1])).then_inc(const_dma, 16)
            sp.dma_start(gates_raw[:, 1:2], gf_d.rearrange("(a n) -> a n", a=1).to_broadcast([P, 1])).then_inc(const_dma, 16)
            sp.dma_start(wg1[:, :], wg1_d).then_inc(const_dma, 16)
            sp.dma_start(wg2[:, :], wg2_d).then_inc(const_dma, 16)

            def step(s, u):
                b, p = s - O_LOAD, (u - O_LOAD) % 2
                if valid(b):
                    wait(sp, q_lo, b - 1)
                    sp.dma_start(x_in[p][:, :], x_d[bass.ds(b, 1), :, :].rearrange("a s d -> (a s) d")).then_inc(x_loaded[p], 16)
                    wait(sp, k_hi, b - 1)
                    wait(sp, k_rem_done, b - 1)
                    wait(sp, v_done, b - 1)
                    sp.dma_start(c_in[p][:, :], ctx_d[bass.ds(b, 1), :, :].rearrange("a s d -> (a s) d")).then_inc(c_loaded[p], 16)
                    wait(sp, w_lo_done, b)
                    sp.dma_start(wst[:, :], w_d[bass.ds(b, 1), :, :].rearrange("a p n -> (a p) n")).then_inc(w_loaded, 16)
                b, p = s - O_ST, (u - O_ST) % 2
                if valid(b):
                    max_rows(b, p, 1)
                    wait(sp, z_done, b - 1)
                    wait(sp, res_stored[p], ring2(b - 2, p))
                    sp.dma_start(x_res[p][:, :], x_d[bass.ds(b, 1), :, :].rearrange("a s d -> (a s) d")).then_inc(res_loaded[p], 16)
                b, p = s - O_S, (u - O_S) % 2
                if valid(b):
                    max_rows(b, p, 0)
                b, p = s - O_OUT, (u - O_OUT) % 2
                if valid(b):
                    sp.wait_ge(res_done, b + 1)
                    sp.dma_start(x2_d[bass.ds(b, 1), :, :].rearrange("a s d -> (a s) d"), x_res[p][:, :]).then_inc(res_stored[p], 16)

            def max_rows(b, p, half):
                sp.wait_ge(mt_copied, 2 * b + half + 1)
                dst = kq[p][:, :].rearrange("r (m s) -> r m s", s=S)
                for j in range(MROWS):
                    sp.dma_start(dst[QROWS + j:QROWS + j + 1, MHALF * half:MHALF * (half + 1), :],
                                 mt_sb[half][MHALF * j:MHALF * (j + 1), :]).then_inc(mrow[half], 16)

            pipeline(sp, step, STEPS, LOOP0, B, RING)
            for p in range(2):
                sp.wait_ge(res_stored[p], ring2(B - 2 + p, p))
            sp.drain().then_inc(phase1_over, 1)
            sp.wait_ge(phase1_over, 5)

            sp.dma_start(bup[:, :], bup_d.to_broadcast([P, E * HE])).then_inc(bias_loaded, 16)
            sp.dma_start(bdn[:, :], bdn_d.to_broadcast([P, E * D])).then_inc(bias_loaded, 16)
            sp.wait_ge(f_const, 3)
            sp.dma_start(slots_d[E * REGION:ROWS, :].rearrange("(t p) d -> p t d", p=P),
                         zeros[:, :].unsqueeze(1).to_broadcast([P, DUMMY, D])).then_inc(dummy_done, 16)
            sp.wait_ge(dummy_done, 16)
            sp.wait_ge(pads_done, 16 * E)
            sp.wait_ge(tab_done, 2)

            def tile_step(s, u):
                t, p = s, u % 2
                if valid(t, TILES):
                    row = sp.value_load(tab_r[0:1, bass.ds(t, 1)], min_val=0, max_val=ROWS - P)
                    wait(sp, ft_done, t - 1)
                    sp.dma_start(z_s[p][:, :], slots_d[bass.ds(row, P), :]).then_inc(tile_loaded[p], 16)
                t, p = s - 4, u % 2
                if valid(t, TILES):
                    sp.wait_ge(y_done, t + 1)
                    sp.dma_start(y_d[bass.ds(t * P, P), :], y_sb[p][:, :]).then_inc(y_stored[p], 16)

            pipeline(sp, tile_step, TILES + 4, 4, 4 + (TILES - 4) // 2 * 2, 2)
            for p in range(2):
                last = TILES - 1 - (TILES - 1 - p) % 2
                sp.wait_ge(y_stored[p], ring2(last, p))
            sp.drain().then_inc(phase2_over, 1)
            sp.wait_ge(phase2_over, 5)

            def mix_step(s, q):
                b = s
                if valid(b):
                    wait(sp, stored[q], ring4(b - RING, q, 16))
                    sp.dma_start(r_in[q][:, :], x2_d[bass.ds(b, 1), :, :].rearrange("a s d -> (a s) d")).then_inc(r_loaded[q], 16)
                b, q = s - 3, (q - 3) % RING
                if valid(b):
                    sp.wait_ge(mix2, b + 1)
                    sp.dma_start(out_d[bass.ds(b, 1), :, :].rearrange("a s d -> (a s) d"), r_in[q][:, :]).then_inc(stored[q], 16)

            pipeline(sp, mix_step, B + 3, 8, B, RING)
            for q in range(RING):
                sp.wait_ge(stored[q], ring4(B - RING + q, q, 16))

        @block.gpsimd
        def _(pool):
            g = nc.gpsimd

            def hold(i, n):
                wait(pool, held[i], n)
                g.tensor_tensor(tock[:, i:i + 1], tick[:, :], tick[:, :], ALU.mult).then_inc(held[i], 1)

            g.memset(ident_f[:, :], 0.0).then_inc(const_ready, 1)
            g.memset(ident_b[:, :], 0.0).then_inc(const_ready, 1)
            g.memset(before[:, :], 0.0).then_inc(const_ready, 1)
            g.memset(ones_b[:, :], 1.0).then_inc(const_ready, 1)
            g.memset(minus_half[:, :], -0.5).then_inc(const_ready, 1)
            g.memset(eps[:, :], EPS).then_inc(const_ready, 1)
            g.memset(tick[:, :], 1.0).then_inc(const_ready, 1)
            for i in range(RING):
                g.memset(v_aug[i][:, :], 0.0).then_inc(const_ready, 1)
            for i in range(2):
                g.memset(nm_parts[i][:, :], 1.0).then_inc(const_ready, 1)
            g.iota(ebase[:, :], [[REGION, E]], base=0, channel_multiplier=0,
                   allow_small_or_imprecise_dtypes=True).then_inc(const_ready, 1)
            g.iota(run[:, :], [[REGION, E]], base=0, channel_multiplier=0,
                   allow_small_or_imprecise_dtypes=True).then_inc(const_ready, 1)
            g.iota(iota_e[:, :], [[1, E]], base=0, channel_multiplier=0,
                   allow_small_or_imprecise_dtypes=True).then_inc(const_ready, 1)
            g.iota(iota_p[:, :], [[1, 1]], base=0, channel_multiplier=1,
                   allow_small_or_imprecise_dtypes=True).then_inc(const_ready, 1)
            pool.wait_ge(const_ready, 17)
            for m in (ident_f, ident_b):
                g.affine_select(out=m[:, :], in_=m[:, :], compare_op=ALU.not_equal, fill=1.0, base=0,
                                pattern=[[-1, P]], channel_multiplier=1).then_inc(const_ready, 1)
            g.affine_select(out=before[:, :], in_=before[:, :], compare_op=ALU.is_ge, fill=1.0, base=0,
                            pattern=[[-1, P]], channel_multiplier=1).then_inc(const_ready, 1)
            last = g.memset(v_aug[0][:, :].rearrange("p (k c) -> p k c", c=32)[:, :, HD:HD + 1], 1.0)
            for i in range(1, RING):
                last = g.memset(v_aug[i][:, :].rearrange("p (k c) -> p k c", c=32)[:, :, HD:HD + 1], 1.0)
            last.then_inc(const_ready, 1)

            def step(s, u):
                b, p = s - O_NORM, (u - O_NORM) % 2
                if valid(b):
                    pool.wait_ge(n_mv, b + 1)
                    g.tensor_tensor(ve_n[:, :], mv_n[:, 1:2], eps[:, :], ALU.add).then_inc(n_ve, 1)
                    pool.wait_ge(n_ve, b + 1)
                    g.tensor_tensor(rs_n[:, :], ve_n[:, :], minus_half[:, :], ALU.pow).then_inc(n_rs, 1)
                    kn = k_nat[p][:, :].rearrange("p (k j d) -> p k j d", j=PARTS, d=HD)
                    rem = k_rem[:, :].rearrange("p (k d) -> p k d", d=HD)
                    pool.wait_ge(k_hi, b + 1)
                    g.tensor_tensor(rem, c_in[p][:, :].rearrange("p (k d) -> p k d", d=HD), kn[:, :, 3, :],
                                    ALU.subtract).then_inc(k_rem_done, 1)
                    pool.wait_ge(k_mid, b + 1)
                    g.tensor_tensor(kn[:, :, 0, :], rem, kn[:, :, 1, :], ALU.subtract).then_inc(k_lo, 1)
                    qn = q_nat[p][:, :].rearrange("p (h j d) -> p h j d", j=4, d=HD)
                    xv = x_in[p][:, :].rearrange("p (h d) -> p h d", d=HD)
                    pool.wait_ge(q_hi, b + 1)
                    g.tensor_tensor(xv, xv, qn[:, :, 1, :], ALU.subtract).then_inc(q_rem, 1)
                    pool.wait_ge(q_mid, b + 1)
                    g.tensor_tensor(qn[:, :, 3, :], xv, qn[:, :, 2, :], ALU.subtract).then_inc(q_lo, 1)
                b, q = s - O_SLOT, (u - O_SLOT) % RING
                if valid(b):
                    pool.wait_ge(sloti_done, b + 1)
                    hold(0, b)
                    for j in range(2):
                        g.indirect_dma_start(
                            out=slots_d, out_offset=bass.IndirectOffsetOnAxis(ap=slot_i[q][:, j:j + 1], axis=0),
                            in_=z[q][:, :], in_offset=None).then_inc(scattered[q], 16)
                b, p, q = s - O_OUT, (u - O_OUT) % 2, (u - O_OUT) % RING
                if valid(b):
                    pool.wait_ge(res_loaded[p], ring2(b, p))
                    pool.wait_ge(att_done, 2 * b + 2)
                    g.tensor_tensor(x_res[p][:, :], x_res[p][:, :], z[q][:, :], ALU.add).then_inc(res_done, 1)
                    pool.wait_ge(o_mv, b + 1)
                    g.tensor_tensor(ve_o[:, :], mv_o[:, 1:2], eps[:, :], ALU.add).then_inc(o_ve, 1)
                    pool.wait_ge(o_ve, b + 1)
                    g.tensor_tensor(rs_o[:, :], ve_o[:, :], minus_half[:, :], ALU.pow).then_inc(o_rs, 1)
                c = s
                if valid(c):
                    pool.wait_ge(w_hi_done, c + 1)
                    g.tensor_tensor(w_lo[:, bass.ds(c * WCHUNK, WCHUNK)], wst[:, :],
                                    w_hi[:, bass.ds(c * WCHUNK, WCHUNK)].bitcast(F32),
                                    ALU.subtract).then_inc(w_lo_done, 1)

            pipeline(pool, step, STEPS, LOOP0, B, RING)
            for q in range(RING):
                pool.wait_ge(scattered[q], ring4(B - RING + q, q, 32))
            pool.drain().then_inc(phase1_over, 1)
            pool.wait_ge(phase1_over, 5)

            g.iota(i128[:, :], [[P, B]], base=0, channel_multiplier=0,
                   allow_small_or_imprecise_dtypes=True).then_inc(f_const, 1)
            g.iota(iota_t[:, :], [[1, TILES]], base=0, channel_multiplier=0,
                   allow_small_or_imprecise_dtypes=True).then_inc(f_const, 1)
            g.memset(zeros[:, :], 0.0).then_inc(f_const, 1)
            pool.wait_ge(f_const, 3)
            pool.wait_ge(pad_idx, 2)
            for e in range(E):
                g.indirect_dma_start(out=slots_d, out_offset=bass.IndirectOffsetOnAxis(ap=pad_i[:, e:e + 1], axis=0),
                                     in_=zeros[:, :], in_offset=None).then_inc(pads_done, 16)
            pool.wait_ge(pads_done, 16 * E)
            pool.drain().then_inc(phase2_over, 1)
            pool.wait_ge(phase2_over, 5)

            def mix_step(s, q):
                b = s
                wait(pool, mix2, b - RING + 1)
                hold(1, b)
                g.tensor_copy(g_idx[q][:, :], rows_all[:, bass.ds(b * 2, 2)]).then_inc(gi_done, 1)
                pool.wait_ge(gi_done, b + 1)
                hold(2, b)
                for j, (y, done) in enumerate(((y1[q], y1_loaded[q]), (y2[q], y2_loaded[q]))):
                    g.indirect_dma_start(out=y[:, :], out_offset=None, in_=y_d,
                                         in_offset=bass.IndirectOffsetOnAxis(ap=g_idx[q][:, j:j + 1], axis=0)
                                         ).then_inc(done, 16)

            pipeline(pool, mix_step, B, 4, B, RING)

        @block.scalar
        def _(act):
            a = nc.scalar
            act.wait_ge(const_dma, 64)
            act.wait_ge(const_ready, 21)
            a.activation(gates[:, :], gates_raw[:, :], ACT.Tanh).then_inc(gate_ready, 1)

            def step(s, u):
                b1, p1_, r1 = s - O_NORM, (u - O_NORM) % 2, (u - O_NORM) % RING
                b2, p2_ = s - O_QT, (u - O_QT) % 2
                b4 = s - O_ST
                b5 = s - O_OUT
                b6 = s - O_GATE
                for k in range(KV):
                    if valid(b4):
                        n = b4 * KV + k
                        act.wait_ge(st_done, n + 1)
                        if k == 0:
                            wait(act, pv_done, 2 * b4 - 1)
                        if k == 4:
                            wait(act, pv_done, 2 * b4)
                        a.activation(probs[:, k * G * S:(k + 1) * G * S], st_ps[k % 2][:, :], ACT.Exp,
                                     scale=HD ** -0.5).then_inc(exp_done, 1)
                    if k % 2 and valid(b2):
                        act.wait_ge(qt_done, b2 * KV + k + 1)
                        wait(act, st_done, (b2 - 2) * KV + k + 1)
                        a.activation(kq[p2_][0:QROWS, k * KQ:(k + 1) * KQ],
                                     qt_ps[k % 2][:, :].bitcast(BF16)[0:QROWS, 0:KQ], ACT.Copy).then_inc(qt_act, 1)
                    if k == 0 and valid(b1):
                        act.wait_ge(c_loaded[p1_], ring2(b1, p1_))
                        wait(act, pv_done, 2 * (b1 - 3))
                        a.activation(v_aug[r1][:, :].rearrange("p (k c) -> p k c", c=32)[:, :, 0:HD],
                                     c_in[p1_][:, :].rearrange("p (k d) -> p k d", d=HD), ACT.Copy).then_inc(v_done, 1)
                    if k == 1 and valid(b5):
                        act.wait_ge(pv_done, 2 * b5 + 2)
                        act.wait_ge(on_done, 2 * b5 + 1)
                        a.activation(o_sb[:, :], bank_a[:, :], ACT.Copy).then_inc(o_copied, 1)
                    if k == 2 and valid(b6):
                        act.wait_ge(zt_done, b6 + 1)
                        wait(act, lg1_done, b6)
                        a.activation(z_t[:, :], bank_b[:, :], ACT.Copy).then_inc(zt_copied, 1)
                    if k == 3 and valid(b1):
                        act.wait_ge(n_done, b1 + 1)
                        wait(act, qt_done, (b1 - 1) * KV)
                        qn = q_nat[p1_][:, :].rearrange("p (h j d) -> p h j d", j=4, d=HD)
                        a.activation(qn[:, :, 0:2, :], x_in[p1_][:, :].rearrange("p (h d) -> p h d", d=HD)
                                     .unsqueeze(2).to_broadcast([P, H, 2, HD]), ACT.Copy).then_inc(q_hi, 1)
                    if k == 4 and valid(b6):
                        act.wait_ge(lg1_done, b6 + 1)
                        wait(act, lg2_done, b6)
                        a.activation(th_sb[:, :], bank_a[0:E, 0:S], ACT.Tanh).then_inc(th_done, 1)
                    if k == 5 and valid(b4):
                        act.wait_ge(pv_done, 2 * b4 + 1)
                        wait(act, on_done, 2 * b4)
                        a.activation(o_sb[:, :], bank_a[:, :], ACT.Copy).then_inc(o_copied, 1)
                    if k == 6 and valid(b1):
                        act.wait_ge(q_rem, b1 + 1)
                        a.activation(qn[:, :, 2, :], x_in[p1_][:, :].rearrange("p (h d) -> p h d", d=HD),
                                     ACT.Copy).then_inc(q_mid, 1)
                    if k == 7 and valid(s):
                        act.wait_ge(w_loaded, 16 * (s + 1))
                        a.activation(w_hi[:, bass.ds(s * WCHUNK, WCHUNK)], wst[:, :], ACT.Copy).then_inc(w_hi_done, 1)

            pipeline(act, step, STEPS, LOOP0, B, RING)
            act.wait_ge(gap_done, B)
            act.drain().then_inc(phase1_over, 1)
            act.wait_ge(phase1_over, 5)
            a.activation(egap[:, :], gap_all[:, :], ACT.Exp).then_inc(exp2_done, 1)

            def tile_step(s, u):
                t, p = s - 3, (u - 3) % 2
                if valid(t, TILES):
                    act.wait_ge(ht_done, t + 1)
                    wait(act, dn_done, t - 1)
                    a.activation(hh[p][:, :], bank[4 + p][:, 0:HE], ACT.Copy).then_inc(hh_done, 1)
                t, p = s - 1, (u - 1) % 2
                if valid(t, TILES):
                    act.wait_ge(ft_done, t + 1)
                    wait(act, up_done, t - 1)
                    a.activation(zh[p][:, :], bank[p][:, :], ACT.Copy).then_inc(zh_done, 1)
                t, p = s - 2, (u - 2) % 2
                if valid(t, TILES):
                    act.wait_ge(u_done, t + 1)
                    wait(act, h_done, t - 1)
                    a.activation(t_sb[p][:, :], u_sb[p][:, :], ACT.Tanh, scale=0.5).then_inc(tanh_done, 1)

            pipeline(act, tile_step, TILES + 4, 4, 4 + (TILES - 4) // 2 * 2, 2)
            act.drain().then_inc(phase2_over, 1)

        @block.vector
        def _(dve):
            v = nc.vector
            dve.wait_ge(const_ready, 21)
            dve.wait_ge(gate_ready, 1)

            def max_parts(b, p, half):
                src = nmax[p][:, H // 2 * half:H // 2 * (half + 1)].rearrange("p (k g) -> p k g", g=G)
                rem = nm_rem[half][:, :].rearrange("p (k g) -> p k g", g=G)
                hi, mid, lo = (nm_parts[half][:, MHALF * j:MHALF * (j + 1)]
                               .rearrange("p (k c) -> p k c", c=G + 1)[:, :, 1:] for j in range(MROWS))
                cnt = 2 * b + half + 1
                wait(dve, mt_done, cnt - 2)
                dve.wait_ge(max_done, KV * b + 4 * half + 4)
                v.tensor_copy(hi, src).then_inc(nm_hi, 1)
                dve.wait_ge(nm_hi, cnt)
                v.tensor_tensor(rem, src, hi, ALU.subtract).then_inc(nm_remd, 1)
                dve.wait_ge(nm_remd, cnt)
                v.tensor_copy(mid, rem).then_inc(nm_mid, 1)
                dve.wait_ge(nm_mid, cnt)
                v.tensor_tensor(lo, rem, mid, ALU.subtract).then_inc(nm_lo, 1)

            def max_copy(b, half, src):
                dve.wait_ge(mt_done, 2 * b + half + 1)
                wait(dve, mrow[half], 16 * MROWS * b)
                v.tensor_copy(mt_sb[half][:, :], src[:, :].bitcast(BF16)[0:MROWS * MHALF, 0:S]).then_inc(mt_copied, 1)

            def attend(b, q, grp):
                cnt = 2 * b + grp + 1
                o = bank_b[:, :].rearrange("p (g k c) -> p g k c", g=G, c=32)
                dve.wait_ge(on_done, cnt)
                v.reciprocal(rden[:, :].rearrange("p (g k) -> p g k", g=G), o[:, :, :, HD]).then_inc(rden_done, 1)
                dve.wait_ge(rden_done, cnt)
                v.tensor_scalar(rgate[:, :], rden[:, :], gates[:, 0:1], None, ALU.mult).then_inc(rgate_done, 1)
                dve.wait_ge(rgate_done, cnt)
                if grp == 0:
                    wait(dve, scattered[q], ring4(b - RING, q, 32))
                v.tensor_tensor(
                    z[q][:, :].rearrange("p (k g d) -> p g k d", g=G, d=HD)[:, :, 4 * grp:4 * grp + 4, :],
                    o[:, :, :, 0:HD],
                    rgate[:, :].rearrange("p (g k) -> p g k", g=G).unsqueeze(3).to_broadcast([P, G, 4, HD]),
                    ALU.mult).then_inc(att_done, 1)

            def step(s, u):
                b1, p1_ = s - O_NORM, (u - O_NORM) % 2
                b2, p2_ = s - O_QT, (u - O_QT) % 2
                b3, p3_ = s - O_S, (u - O_S) % 2
                b4 = s - O_ST
                b5, p5_, q5 = s - O_OUT, (u - O_OUT) % 2, (u - O_OUT) % RING
                b6, p6_, q6 = s - O_GATE, (u - O_GATE) % 2, (u - O_GATE) % RING
                b7, p7_ = s - O_ROUTE, (u - O_ROUTE) % 2
                b8, p8_, q8 = s - O_SLOT, (u - O_SLOT) % 2, (u - O_SLOT) % RING
                if valid(b6):
                    dve.wait_ge(o_rs, b6 + 1)
                    v.tensor_scalar(z[q6][:, :], x_res[p6_][:, :], mv_o[:, 0:1], rs_o[:, :], ALU.subtract,
                                    ALU.mult).then_inc(z_done, 1)
                for k in range(KV):
                    if valid(b3):
                        n = b3 * KV + k
                        dve.wait_ge(s_done, n + 1)
                        v.tensor_reduce(nmax[p3_][:, k * G:(k + 1) * G],
                                        s_ps[k % 2][:, :].rearrange("p (g t) -> p g t", g=G),
                                        X_AXIS, ALU.max, negate=True).then_inc(max_done, 1)
                    if k % 2 == 0 and valid(b2):
                        dve.wait_ge(qt_done, b2 * KV + k + 1)
                        wait(dve, st_done, (b2 - 2) * KV + k + 1)
                        v.tensor_copy(kq[p2_][0:QROWS, k * KQ:(k + 1) * KQ],
                                      qt_ps[k % 2][:, :].bitcast(BF16)[0:QROWS, 0:KQ]).then_inc(qt_dve, 1)
                    if k == 0:
                        if valid(b4):
                            max_copy(b4, 1, bank_a)
                        if valid(b1):
                            dve.wait_ge(x_loaded[p1_], ring2(b1, p1_))
                            v.bn_stats(st_n[:, :], x_in[p1_][:, :]).then_inc(n_stats, 1)
                        if valid(b7):
                            v.max(top8[:, :], lg_sb[p7_][:, :]).then_inc(top_done, 1)
                        if valid(b8):
                            dve.wait_ge(pos_done, b8 + 1)
                            v.tensor_tensor_reduce(out=junk[:, 0:E], in0=m1[p8_][:, :], in1=pos[:, :], scale=1.0,
                                                   scalar=0.0, op0=ALU.mult, op1=ALU.add,
                                                   accum_out=slot_f[:, 0:1]).then_inc(slot_done, 1)
                        if valid(b1):
                            dve.wait_ge(c_loaded[p1_], ring2(b1, p1_))
                            wait(dve, qt_done, (b1 - 1) * KV)
                            dve.wait_ge(n_stats, b1 + 1)
                            kn = k_nat[p1_][:, :].rearrange("p (k j d) -> p k j d", j=PARTS, d=HD)
                            v.tensor_copy(kn[:, :, 2:5, :], c_in[p1_][:, :].rearrange("p (k d) -> p k d", d=HD)
                                          .unsqueeze(2).to_broadcast([P, KV, 3, HD])).then_inc(k_hi, 1)
                            v.bn_aggr(mv_n[:, :], st_n[:, :]).then_inc(n_mv, 1)
                    if k == 1:
                        if valid(b5):
                            attend(b5, q5, 0)
                        if valid(b8):
                            v.tensor_tensor_reduce(out=junk[:, E:2 * E], in0=m2[p8_][:, :], in1=pos[:, :], scale=1.0,
                                                   scalar=0.0, op0=ALU.mult, op1=ALU.add,
                                                   accum_out=slot_f[:, 1:2]).then_inc(slot_done, 1)
                        if valid(b7):
                            dve.wait_ge(top_done, b7 + 1)
                            v.tensor_tensor(gap_all[:, bass.ds(b7, 1)], top8[:, 1:2], top8[:, 0:1],
                                            ALU.subtract).then_inc(gap_done, 1)
                            v.max_index(idx8[:, :], top8[:, :], lg_sb[p7_][:, :]).then_inc(idx_done, 1)
                    if k == 2:
                        if valid(b1):
                            dve.wait_ge(n_rs, b1 + 1)
                            v.tensor_scalar(x_in[p1_][:, :], x_in[p1_][:, :], mv_n[:, 0:1], rs_n[:, :], ALU.subtract,
                                            ALU.mult).then_inc(n_done, 1)
                        if valid(b8):
                            dve.wait_ge(slot_done, 2 * b8 + 2)
                            v.tensor_copy(slot_i[q8][:, :], slot_f[:, :]).then_inc(sloti_done, 1)
                            v.tensor_copy(slot_all[:, bass.ds(b8 * 2, 2)], slot_f[:, :]).then_inc(slotall_done, 1)
                        if valid(b7):
                            dve.wait_ge(idx_done, b7 + 1)
                            v.tensor_copy(idxf[:, :], idx8[:, 0:2]).then_inc(idxf_done, 1)
                    if k == 3:
                        if valid(b7):
                            dve.wait_ge(idxf_done, b7 + 1)
                            v.tensor_scalar(m1[p7_][:, :], iota_e[:, :], idxf[:, 0:1], None,
                                            ALU.is_equal).then_inc(masks_done, 1)
                            v.tensor_scalar(m2[p7_][:, :], iota_e[:, :], idxf[:, 1:2], None,
                                            ALU.is_equal).then_inc(masks_done, 1)
                        if valid(b3):
                            max_parts(b3, p3_, 0)
                    if k == 4:
                        if valid(b5):
                            attend(b5, q5, 1)
                        if valid(b7):
                            dve.wait_ge(masks_done, 2 * b7 + 2)
                            v.tensor_tensor(m12[p7_][:, :], m1[p7_][:, :], m2[p7_][:, :], ALU.add).then_inc(m12_done, 1)
                    if k == 5 and valid(b1):
                        dve.wait_ge(k_rem_done, b1 + 1)
                        v.tensor_copy(kn[:, :, 1:6:4, :], k_rem[:, :].rearrange("p (k d) -> p k d", d=HD)
                                      .unsqueeze(2).to_broadcast([P, KV, 2, HD])).then_inc(k_mid, 1)
                    if k == 6 and valid(b3):
                        max_copy(b3, 0, bank_b)
                    if k == 7:
                        if valid(b5):
                            dve.wait_ge(res_done, b5 + 1)
                            v.bn_stats(st_o[:, :], x_res[p5_][:, :]).then_inc(o_stats, 1)
                        if valid(b3):
                            max_parts(b3, p3_, 1)
                        if valid(b5):
                            dve.wait_ge(o_stats, b5 + 1)
                            v.tensor_copy(junk[:, 2 * E:2 * E + 2], st_o[:, 0:2])
                            v.bn_aggr(mv_o[:, :], st_o[:, :]).then_inc(o_mv, 1)
                        if valid(b7):
                            dve.wait_ge(rank_done, b7 + 1)
                            wait(dve, run_done, b7)
                            v.tensor_tensor(pos[:, :], bank_b[:, 0:E], run[:, :], ALU.add).then_inc(pos_done, 1)
                            v.tensor_tensor(run[:, :], run[:, :], bank_b[:, E:2 * E], ALU.add).then_inc(run_done, 1)
                        if valid(b6):
                            dve.wait_ge(lg2_done, b6 + 1)
                            v.tensor_copy(lg_sb[p6_][:, :], bank_a[:, 0:E]).then_inc(lg_copied, 1)

            def step_in_order(s, u):
                if valid(s - O_ROUTE):
                    dve.wait_ge(lg_copied, s - O_ROUTE + 1)
                step(s, u)

            pipeline(dve, step_in_order, STEPS, LOOP0, B, RING)
            dve.wait_ge(run_done, B)
            dve.drain().then_inc(phase1_over, 1)
            dve.wait_ge(phase1_over, 5)

            link = [0]

            def then(ins):
                link[0] += 1
                ins.then_inc(tab_step, 1)
                dve.wait_ge(tab_step, link[0])

            v.tensor_scalar(pad_f[:, :], run[:, :], iota_p[:, :], None, ALU.add).then_inc(pad_idx, 1)
            dve.wait_ge(pad_idx, 1)
            v.tensor_copy(pad_i[:, :], pad_f[:, :]).then_inc(pad_idx, 1)
            then(v.tensor_tensor(count[:, :], run[:, :], ebase[:, :], ALU.subtract))
            dve.wait_ge(f_const, 2)
            ov = over[:, :].rearrange("p (e i) -> p e i", e=E)
            then(v.tensor_tensor(ov, count[:, :].unsqueeze(2).to_broadcast([P, E, B]),
                                 i128[:, :].unsqueeze(1).to_broadcast([P, E, B]), ALU.is_gt))
            then(v.tensor_reduce(ntile[:, :], ov, X_AXIS, ALU.add))
            then(v.tensor_copy(tend[:, 0:1], ntile[:, 0:1]))
            for e in range(1, E):
                then(v.tensor_tensor(tend[:, e:e + 1], tend[:, e - 1:e], ntile[:, e:e + 1], ALU.add))
            then(v.tensor_scalar(tskip[:, :], ntile[:, :], float(-P), float(REGION), ALU.mult, ALU.add))
            pv_ = past[:, :].rearrange("p (t e) -> p t e", e=E)
            pw_ = pastw[:, :].rearrange("p (t e) -> p t e", e=E)
            then(v.tensor_tensor(pv_, iota_t[:, :].unsqueeze(2).to_broadcast([P, TILES, E]),
                                 tend[:, :].unsqueeze(1).to_broadcast([P, TILES, E]), ALU.is_ge))
            then(v.tensor_reduce(tile_e[:, :], pv_, X_AXIS, ALU.add))
            then(v.tensor_tensor(pw_, pv_, tskip[:, :].unsqueeze(1).to_broadcast([P, TILES, E]), ALU.mult))
            then(v.tensor_reduce(tile_r[:, :], pw_, X_AXIS, ALU.add))
            v.tensor_scalar(tab_e[:, :], tile_e[:, :], float(E - 1), None, ALU.min).then_inc(tab_done, 1)
            v.scalar_tensor_tensor(tab_r[:, :], iota_t[:, :], float(P), tile_r[:, :], ALU.mult,
                                   ALU.add).then_inc(tab_done, 1)
            then(v.tensor_scalar(drop[:, 0:1], tskip[:, 0:1], 0.0, None, ALU.mult))
            then(v.tensor_copy(drop[:, 1:E], tskip[:, 0:E - 1]))
            bv = beyond[:, :].rearrange("p (n e) -> p n e", e=E)
            then(v.tensor_tensor(bv, slot_all[:, :].unsqueeze(2).to_broadcast([P, 2 * B, E]),
                                 ebase[:, :].unsqueeze(1).to_broadcast([P, 2 * B, E]), ALU.is_ge))
            then(v.tensor_tensor(bv, bv, drop[:, :].unsqueeze(1).to_broadcast([P, 2 * B, E]), ALU.mult))
            then(v.tensor_reduce(shift[:, :], bv, X_AXIS, ALU.add))
            then(v.tensor_tensor(rows_all[:, :], slot_all[:, :], shift[:, :], ALU.subtract))
            dve.wait_ge(exp2_done, 1)
            then(v.tensor_scalar(sden[:, :], egap[:, :], 1.0, None, ALU.add))
            then(v.reciprocal(sden[:, :], sden[:, :]))
            then(v.tensor_scalar(coef[0][:, :], sden[:, :], gates[:, 1:2], 0.5, ALU.mult, ALU.mult))
            v.tensor_tensor(coef[1][:, :], coef[0][:, :], egap[:, :], ALU.mult).then_inc(coef_step, 1)
            dve.wait_ge(bias_loaded, 32)
            then(v.tensor_scalar(bdn[:, :], bdn[:, :], 2.0, None, ALU.mult))
            dve.wait_ge(tab_done, 2)

            def tile_step(s, u):
                t, p = s - 3, (u - 3) % 2
                if valid(t, TILES):
                    dve.wait_ge(hh_done, t + 1)
                    wait(dve, dn_done, t - 1)
                    v.tensor_tensor(hl[p][:, :], bank[4 + p][:, 0:HE], hh[p][:, :].bitcast(F32),
                                    ALU.subtract).then_inc(hl_done, 1)
                t, p = s - 1, (u - 1) % 2
                if valid(t, TILES):
                    dve.wait_ge(zh_done, t + 1)
                    wait(dve, up_done, t - 1)
                    v.tensor_tensor(zl[p][:, :], bank[p][:, :], zh[p][:, :].bitcast(F32),
                                    ALU.subtract).then_inc(zl_done, 1)
                t, p = s - 2, (u - 2) % 2
                if valid(t, TILES):
                    e = dve.value_load(tab_e[0:1, bass.ds(t, 1)], min_val=0, max_val=E - 1)
                    dve.wait_ge(up_done, t + 1)
                    wait(dve, tanh_done, t - 1)
                    v.tensor_tensor(u_sb[p][:, :], bank[2 + p][:, 0:HE], bup[:, bass.ds(e * HE, HE)],
                                    ALU.add).then_inc(u_done, 1)
                    dve.wait_ge(tanh_done, t + 1)
                    wait(dve, ht_done, t - 1)
                    v.scalar_tensor_tensor(h_sb[p][:, :], t_sb[p][:, :], 1.0, u_sb[p][:, :], ALU.add,
                                           ALU.mult).then_inc(h_done, 1)
                t, p = s - 3, (u - 3) % 2
                if valid(t, TILES):
                    e = dve.value_load(tab_e[0:1, bass.ds(t, 1)], min_val=0, max_val=E - 1)
                    dve.wait_ge(dn_done, t + 1)
                    wait(dve, y_stored[p], ring2(t - 2, p))
                    v.tensor_tensor(y_sb[p][:, :], bank[6 + p][:, :], bdn[:, bass.ds(e * D, D)],
                                    ALU.add).then_inc(y_done, 1)

            pipeline(dve, tile_step, TILES + 4, 4, 4 + (TILES - 4) // 2 * 2, 2)
            dve.drain().then_inc(phase2_over, 1)

            def mix_step(s, q):
                b = s
                dve.wait_ge(r_loaded[q], ring4(b, q, 16))
                dve.wait_ge(y1_loaded[q], ring4(b, q, 16))
                v.scalar_tensor_tensor(r_in[q][:, :], y1[q][:, :], coef[0][:, bass.ds(b, 1)], r_in[q][:, :],
                                       ALU.mult, ALU.add).then_inc(mix1, 1)
                dve.wait_ge(mix1, b + 1)
                dve.wait_ge(y2_loaded[q], ring4(b, q, 16))
                v.scalar_tensor_tensor(r_in[q][:, :], y2[q][:, :], coef[1][:, bass.ds(b, 1)], r_in[q][:, :],
                                       ALU.mult, ALU.add).then_inc(mix2, 1)

            pipeline(dve, mix_step, B, 4, B, RING)

        @block.tensor
        def _(pe):
            t_ = nc.tensor
            pe.wait_ge(const_ready, 21)
            pe.wait_ge(const_dma, 64)

            def step(s, u):
                b2, p2_ = s - O_QT, (u - O_QT) % 2
                b3, p3_ = s - O_S, (u - O_S) % 2
                b4, p4_, r4 = s - O_ST, (u - O_ST) % 2, (u - O_ST) % RING
                b5, r5 = s - O_OUT, (u - O_OUT) % RING
                b6, q6 = s - O_GATE, (u - O_GATE) % RING
                b7, p7_ = s - O_ROUTE, (u - O_ROUTE) % 2
                b8 = s - O_SLOT

                def weighted_sum(b, r, grp):
                    for j in range(4):
                        k = 4 * grp + j
                        last = t_.matmul(bank_a[32 * j:32 * j + 32, :], v_aug[r][:, 32 * k:32 * k + 32],
                                         probs[:, k * G * S:(k + 1) * G * S], start=True, stop=True,
                                         tile_position=(0, 32 * j))
                    last.then_inc(pv_done, 1)

                def rows_back(b, grp):
                    pe.wait_ge(o_copied, 2 * b + grp + 1)
                    for g_ in range(G):
                        last = t_.transpose(bank_b[:, P * g_:P * g_ + P], o_sb[:, S * g_:S * g_ + S], ident_f[:, :])
                    last.then_inc(on_done, 1)

                def turn_maxima(b, half, dst):
                    pe.wait_ge(nm_lo, 2 * b + half + 1)
                    t_.transpose(dst[:, :].bitcast(BF16)[0:MWIDE, 0:S], nm_parts[half][:, :],
                                 ident_b[:, :]).then_inc(mt_done, 1)

                for k in range(KV):
                    if k == 0:
                        if valid(b5):
                            if valid(b8):
                                pe.wait_ge(run_done, b8 + 1)
                            elif valid(s - 4):
                                wait(pe, mt_copied, 2 * (s - 4) + 1)
                            rows_back(b5, 0)
                        if valid(b4):
                            if valid(b7):
                                pe.wait_ge(lg_copied, b7 + 1)
                            elif valid(b5):
                                pe.wait_ge(o_copied, 2 * b5 + 1)
                            turn_maxima(b4, 1, bank_a)
                    if valid(b4):
                        if k % 4 == 0:
                            pe.wait_ge(mrow[k // 4], 16 * MROWS * (b4 + 1))
                        wait(pe, exp_done, b4 * KV + (k - 1))
                        c = k * KQ
                        t_.matmul(st_ps[k % 2][:, :], kq[p4_][0:QROWS + MROWS, c:c + P],
                                  kq[p4_][0:QROWS + MROWS, c + P:c + KQ], start=True, stop=True).then_inc(st_done, 1)
                    if valid(b2):
                        if k == 0:
                            pe.wait_ge(q_lo, b2 + 1)
                            pe.wait_ge(k_lo, b2 + 1)
                        if k % 2 == 0:
                            wait(pe, qt_dve, b2 * 4 + k // 2)
                        else:
                            wait(pe, qt_act, b2 * 4 + k // 2)
                        dst = qt_ps[k % 2][:, :].bitcast(BF16)
                        t_.transpose(dst[0:QROWS, 0:P], k_nat[p2_][:, k * QROWS:(k + 1) * QROWS], ident_b[:, :])
                        for g_ in range(G):
                            h = k * G + g_
                            c0, cols = h * 4 * HD, slice(P + P * g_, 2 * P + P * g_)
                            t_.transpose(dst[0:4 * HD, cols], q_nat[p2_][:, c0:c0 + 4 * HD], ident_b[:, :])
                            last = t_.transpose(dst[4 * HD:QROWS, cols], q_nat[p2_][:, c0 + HD:c0 + 3 * HD],
                                                ident_b[:, :], tile_position=(0, 4 * HD))
                        last.then_inc(qt_done, 1)
                    if valid(b3):
                        if k % 2 == 0:
                            pe.wait_ge(qt_dve, b3 * 4 + k // 2 + 1)
                        else:
                            pe.wait_ge(qt_act, b3 * 4 + k // 2 + 1)
                        wait(pe, max_done, b3 * KV + (k - 1))
                        c = k * KQ
                        for g_ in range(G):
                            last = t_.matmul(s_ps[k % 2][:, P * g_:P * g_ + P],
                                             kq[p3_][0:QROWS, c + P + P * g_:c + 2 * P + P * g_],
                                             kq[p3_][0:QROWS, c:c + P], start=True, stop=True)
                        last.then_inc(s_done, 1)
                    if k == 1 and valid(b5):
                        pe.wait_ge(exp_done, KV * b5 + KV)
                        if valid(b4):
                            pe.wait_ge(mt_copied, 2 * b4 + 2)
                        else:
                            pe.wait_ge(lg_copied, b7 + 1)
                        weighted_sum(b5, r5, 1)
                    if k == 2 and valid(b6):
                        pe.wait_ge(z_done, b6 + 1)
                        if valid(b5):
                            pe.wait_ge(att_done, 2 * b5 + 1)
                        else:
                            pe.wait_ge(run_done, b8 + 1)
                        for c in range(DC):
                            last = t_.transpose(bank_b[:, P * c:P * c + P], z[q6][:, P * c:P * c + P], ident_f[:, :])
                        last.then_inc(zt_done, 1)
                    if k == 3 and valid(b5):
                        if valid(b6):
                            pe.wait_ge(zt_copied, b6 + 1)
                        else:
                            pe.wait_ge(att_done, 2 * b5 + 1)
                        rows_back(b5, 1)
                    if k == 4 and valid(b6):
                        pe.wait_ge(zt_copied, b6 + 1)
                        if valid(b5):
                            pe.wait_ge(o_copied, 2 * b5 + 2)
                        else:
                            pe.wait_ge(lg_copied, b7 + 1)
                        for c in range(DC):
                            last = t_.matmul(bank_a[0:E, 0:S], wg1[:, c * E:(c + 1) * E], z_t[:, P * c:P * c + P],
                                             start=(c == 0), stop=(c == DC - 1))
                        last.then_inc(lg1_done, 1)
                    if k == 5 and valid(b4):
                        pe.wait_ge(exp_done, KV * b4 + 4)
                        pe.wait_ge(v_done, b4 + 1)
                        if valid(b6):
                            pe.wait_ge(th_done, b6 + 1)
                        elif valid(b5):
                            pe.wait_ge(o_copied, 2 * b5 + 2)
                        else:
                            pe.wait_ge(mt_copied, 2 * b4 + 2)
                        weighted_sum(b4, r4, 0)
                    if k == 6 and valid(b3):
                        if valid(b5):
                            pe.wait_ge(att_done, 2 * b5 + 2)
                        elif valid(b4):
                            wait(pe, mt_copied, 2 * b4 + 1)
                        turn_maxima(b3, 0, bank_b)
                    if k == 7:
                        if valid(b6):
                            pe.wait_ge(th_done, b6 + 1)
                            if valid(b4):
                                pe.wait_ge(o_copied, 2 * b4 + 1)
                            t_.matmul(bank_a[:, 0:E], th_sb[:, :], wg2[:, :], start=True, stop=True).then_inc(lg2_done, 1)
                        if valid(b7):
                            pe.wait_ge(m12_done, b7 + 1)
                            if valid(b3):
                                pe.wait_ge(mt_copied, 2 * b3 + 1)
                            elif valid(b5):
                                pe.wait_ge(att_done, 2 * b5 + 2)
                            elif valid(b6):
                                pe.wait_ge(zt_copied, b6 + 1)
                            else:
                                pe.wait_ge(run_done, b7)
                            t_.matmul(bank_b[:, 0:E], before[:, :], m12[p7_][:, :], start=True, stop=True)
                            t_.matmul(bank_b[:, E:2 * E], ones_b[:, :], m12[p7_][:, :], start=True,
                                      stop=True).then_inc(rank_done, 1)

            pipeline(pe, step, STEPS, LOOP0, B, RING)
            pe.drain().then_inc(phase1_over, 1)
            pe.wait_ge(phase1_over, 5)
            pe.wait_ge(tab_done, 2)

            def tile_step(s, u):
                t, p = s - 3, (u - 3) % 2
                if valid(t, TILES):
                    pe.wait_ge(h_done, t + 1)
                    wait(pe, hl_done, t - 1)
                    for c in range(HC):
                        last = t_.transpose(bank[4 + p][:, P * c:P * c + P], h_sb[p][:, P * c:P * c + P], ident_f[:, :])
                    last.then_inc(ht_done, 1)
                t, p = s - 1, (u - 1) % 2
                if valid(t, TILES):
                    pe.wait_ge(tile_loaded[p], ring2(t, p))
                    wait(pe, zl_done, t - 1)
                    for c in range(DC):
                        last = t_.transpose(bank[p][:, P * c:P * c + P], z_s[p][:, P * c:P * c + P], ident_f[:, :])
                    last.then_inc(ft_done, 1)
                t, p = s - 2, (u - 2) % 2
                if valid(t, TILES):
                    e = pe.value_load(tab_e[0:1, bass.ds(t, 1)], min_val=0, max_val=E - 1)
                    pe.wait_ge(zl_done, t + 1)
                    wait(pe, u_done, t - 1)
                    o = bank[2 + p][:, 0:HE]
                    for c in range(DC):
                        cols = bass.ds(e * (DC * HE) + c * HE, HE)
                        t_.matmul(o, zh[p][:, P * c:P * c + P], w_hi[:, cols], start=(c == 0), stop=False)
                        t_.matmul(o, zh[p][:, P * c:P * c + P], w_lo[:, cols], start=False, stop=False)
                        last = t_.matmul(o, zl[p][:, P * c:P * c + P], w_hi[:, cols], start=False, stop=(c == DC - 1))
                    last.then_inc(up_done, 1)
                t, p = s - 3, (u - 3) % 2
                if valid(t, TILES):
                    e = pe.value_load(tab_e[0:1, bass.ds(t, 1)], min_val=0, max_val=E - 1)
                    pe.wait_ge(hl_done, t + 1)
                    wait(pe, y_done, t - 1)
                    for c in range(HC):
                        cols = bass.ds(e * (HC * D) + (DOWN0 + c * D), D)
                        o = bank[6 + p][:, :]
                        t_.matmul(o, hh[p][:, P * c:P * c + P], w_hi[:, cols], start=(c == 0), stop=False)
                        t_.matmul(o, hh[p][:, P * c:P * c + P], w_lo[:, cols], start=False, stop=False)
                        last = t_.matmul(o, hl[p][:, P * c:P * c + P], w_hi[:, cols], start=False, stop=(c == HC - 1))
                    last.then_inc(dn_done, 1)

            pipeline(pe, tile_step, TILES + 4, 4, 4 + (TILES - 4) // 2 * 2, 2)
            pe.drain().then_inc(phase2_over, 1)


_INS = ["x", "ctx_512", "g_xattn", "g_ffn", "wg1", "wg2", "w", "bup", "bdn"]


def kernel(x, ctx_512, g_xattn, g_ffn, L0_ffn_Wg1, L0_ffn_Wg2, L0_ffn_Wup, L0_ffn_bup, L0_ffn_Wdown, L0_ffn_bdown):
    import numpy as np
    import concourse.bacc as bacc
    from concourse.bass_utils import run_bass_kernel_spmd

    wup, wdown = np.asarray(L0_ffn_Wup), np.asarray(L0_ffn_Wdown)
    up = wup.reshape(E, HE, DC, P).transpose(3, 0, 2, 1).reshape(P, DOWN0)
    down = wdown.reshape(E, D, HC, P).transpose(3, 0, 2, 1).reshape(P, WCOLS - DOWN0)
    w = np.concatenate([up, down], axis=1).reshape(P, WCOLS // WCHUNK, WCHUNK).transpose(1, 0, 2)
    data = {
        "x": x, "ctx_512": ctx_512, "g_xattn": g_xattn, "g_ffn": g_ffn,
        "wg1": np.asarray(L0_ffn_Wg1).reshape(E, DC, P).transpose(2, 1, 0).reshape(P, DC * E),
        "wg2": np.asarray(L0_ffn_Wg2).T,
        "w": w,
        "bup": np.asarray(L0_ffn_bup).reshape(1, E * HE),
        "bdn": np.asarray(L0_ffn_bdown).reshape(1, E * D),
    }
    nc = bacc.Bacc("TRN2", target_bir_lowering=False, num_devices=1)
    arrays, args = {}, []
    for name in _INS:
        a = np.ascontiguousarray(data[name])
        arrays[f"in_{name}"] = a
        args.append(nc.dram_tensor(f"in_{name}", a.shape, mybir.dt.from_np(a.dtype), kind="ExternalInput").ap())
    out = nc.dram_tensor("out", (B, S, D), F32, kind="ExternalOutput").ap()
    block_kernel(nc, *args, out)
    r = run_bass_kernel_spmd(nc, [arrays], core_ids=[0])
    return r.results[0]["out"]
```

```python
import concourse.bass as bass
from concourse import mybir
from contextlib import ExitStack

F32 = mybir.dt.float32
F32R = mybir.dt.float32r
BF16 = mybir.dt.bfloat16
I32 = mybir.dt.int32
U32 = mybir.dt.uint32
ALU = mybir.AluOpType
ACT = mybir.ActivationFunctionType
X_AXIS = mybir.AxisListType.X

P = 128
B, S, D = 32, 128, 512
KV, G, HD = 8, 4, 16
H = KV * G
E, HE = 8, 256
DC, HC = D // P, HE // P
PARTS = 6
QROWS = PARTS * HD
MROWS = 3
MHALF = KV // 2 * (G + 1)
MWIDE = 68
KQ = P + G * P
REGION = B * S + P
TILES = 2 * B * S // P + E - 1
DUMMY = E - 1
ROWS = E * REGION + DUMMY * P
WCHUNK = 512
WCOLS = E * (DC * HE + HC * D)
DOWN0 = E * DC * HE
EPS = 1e-5
O_LOAD, O_NORM, O_QT, O_S, O_ST, O_OUT, O_GATE, O_ROUTE, O_SLOT = range(9)
STEPS = B + O_SLOT
LOOP0 = 12
RING = 4


def valid(b, n=B):
    return not isinstance(b, int) or 0 <= b < n


def wait(eng, sem, value):
    if not isinstance(value, int) or value > 0:
        eng.wait_ge(sem, value)


def pipeline(eng, step, steps, first, last, unroll):
    for s in range(first):
        step(s, s % unroll)
    with eng.Fori(0, (last - first) // unroll) as i:
        for u in range(unroll):
            step(i * unroll + (first + u), (first + u) % unroll)
    for s in range(last, steps):
        step(s, s % unroll)


def tile_pipeline(eng, step):
    first, unroll = 8, 4
    last = first + (TILES - first) // unroll * unroll
    for s in range(first):
        step(s, s % unroll, s == 0)
    with eng.Fori(0, (last - first) // unroll) as i:
        for u in range(unroll):
            step(i * unroll + (first + u), u, u == 0)
    for s in range(last, TILES + 4):
        step(s, s % unroll, s == last)


def block_kernel(nc, x_d, ctx_d, gx_d, gf_d, wg1_d, wg2_d, w_d, bup_d, bdn_d, out_d):
    slots_d = nc.dram_tensor("slots", (ROWS, D), F32, kind="Internal").ap()
    y_d = nc.dram_tensor("expert_out", (TILES * P, D), F32, kind="Internal").ap()
    x2_d = nc.dram_tensor("x2_scratch", (B, S, D), F32, kind="Internal").ap()

    top = ExitStack()
    with top:
        def sb(name, shape, dt, stack=top):
            return stack.enter_context(nc.sbuf_tensor(name, shape, dt))

        def sem(name):
            return top.enter_context(nc.semaphore(name))

        w_hi = sb("w_hi", [P, WCOLS], F32R)
        w_lo = sb("w_lo", [P, WCOLS], F32R)
        slot_all = sb("slot_all", [P, 2 * B], F32)
        rows_all = sb("rows_all", [P, 2 * B], I32)
        gap_all = sb("gap_all", [P, B], F32)
        run = sb("run", [P, E], F32)
        ebase = sb("ebase", [P, E], F32)
        tick = sb("tick", [P, 1], F32)
        tock = sb("tock", [P, 3], F32)
        iota_p = sb("iota_p", [P, 1], F32)
        ident_f = sb("ident_f", [P, P], F32)
        gates = sb("gates", [P, 2], F32)
        gates_raw = sb("gates_raw", [P, 2], F32)

        p1 = ExitStack()
        wst = sb("wst", [P, WCHUNK], F32, p1)
        x_in = [sb(f"x_in{i}", [P, D], F32, p1) for i in range(2)]
        c_in = [sb(f"c_in{i}", [P, P], F32, p1) for i in range(2)]
        q_nat = [sb(f"q_nat{i}", [P, H * 4 * HD], BF16, p1) for i in range(2)]
        k_nat = [sb(f"k_nat{i}", [P, KV * QROWS], BF16, p1) for i in range(2)]
        k_rem = sb("k_rem", [P, P], F32, p1)
        v_aug = [sb(f"v_aug{i}", [P, KV * 32], F32, p1) for i in range(RING)]
        kq = [sb(f"kq{i}", [P, KV * KQ], BF16, p1) for i in range(2)]
        probs = sb("probs", [P, KV * G * S], F32, p1)
        o_sb = sb("o_sb", [P, G * S], F32, p1)
        x_res = [sb(f"x_res{i}", [P, D], F32, p1) for i in range(2)]
        z = [sb(f"z{i}", [P, D], F32, p1) for i in range(RING)]
        z_t = sb("z_t", [P, D], F32, p1)
        nmax = [sb(f"nmax{i}", [P, H], F32, p1) for i in range(2)]
        nm_rem = [sb(f"nm_rem{i}", [P, H // 2], F32, p1) for i in range(2)]
        nm_parts = [sb(f"nm_parts{i}", [P, MWIDE], BF16, p1) for i in range(2)]
        mt_sb = [sb(f"mt_sb{i}", [MROWS * MHALF, S], BF16, p1) for i in range(2)]
        ident_b = sb("ident_b", [P, P], BF16, p1)
        before = sb("before", [P, P], BF16, p1)
        ones_b = sb("ones_b", [P, P], BF16, p1)
        iota_e = sb("iota_e", [P, E], F32, p1)
        wg1 = sb("wg1", [P, DC * E], F32, p1)
        wg2 = sb("wg2", [E, E], F32, p1)
        st_n = sb("st_n", [P, 6], F32, p1)
        mv_n = sb("mv_n", [P, 2], F32, p1)
        ve_n = sb("ve_n", [P, 1], F32, p1)
        rs_n = sb("rs_n", [P, 1], F32, p1)
        st_o = sb("st_o", [P, 6], F32, p1)
        mv_o = sb("mv_o", [P, 2], F32, p1)
        ve_o = sb("ve_o", [P, 1], F32, p1)
        rs_o = sb("rs_o", [P, 1], F32, p1)
        minus_half = sb("minus_half", [P, 1], F32, p1)
        eps = sb("eps", [P, 1], F32, p1)
        rden = sb("rden", [P, G * 4], F32, p1)
        th_sb = sb("th_sb", [E, S], F32, p1)
        lg_sb = [sb(f"lg_sb{i}", [P, E], F32, p1) for i in range(2)]
        top8 = sb("top8", [P, E], F32, p1)
        idx8 = sb("idx8", [P, E], U32, p1)
        idxf = sb("idxf", [P, 2], F32, p1)
        m1 = [sb(f"m1_{i}", [P, E], F32, p1) for i in range(2)]
        m2 = [sb(f"m2_{i}", [P, E], F32, p1) for i in range(2)]
        m12 = [sb(f"m12_{i}", [P, E], BF16, p1) for i in range(2)]
        pos = sb("pos", [P, E], F32, p1)
        junk = sb("junk", [P, 3 * E], F32, p1)
        slot_f = sb("slot_f", [P, 2], F32, p1)
        slot_i = [sb(f"slot_i{i}", [P, 2], I32, p1) for i in range(RING)]
        p1.close()

        p2 = ExitStack()
        bup = sb("bup", [P, E * HE], F32, p2)
        bdn = sb("bdn", [P, E * D], F32, p2)
        z_s = [sb(f"z_s{i}", [P, D], F32, p2) for i in range(2)]
        zh = [sb(f"zh{i}", [P, D], F32R, p2) for i in range(2)]
        zl = [sb(f"zl{i}", [P, D], F32R, p2) for i in range(2)]
        u_sb = [sb(f"u_sb{i}", [P, HE], F32, p2) for i in range(2)]
        t_sb = [sb(f"t_sb{i}", [P, HE], F32, p2) for i in range(2)]
        h_sb = [sb(f"h_sb{i}", [P, HE], F32, p2) for i in range(2)]
        hh = [sb(f"hh{i}", [P, HE], F32R, p2) for i in range(2)]
        hl = [sb(f"hl{i}", [P, HE], F32R, p2) for i in range(2)]
        y_sb = [sb(f"y_sb{i}", [P, D], F32, p2) for i in range(2)]
        zeros = sb("zeros", [P, D], F32, p2)
        count = sb("count", [P, E], F32, p2)
        i128 = sb("i128", [P, B], F32, p2)
        over = sb("over", [P, E * B], F32, p2)
        ntile = sb("ntile", [P, E], F32, p2)
        tend = sb("tend", [P, E], F32, p2)
        tskip = sb("tskip", [P, E], F32, p2)
        iota_t = sb("iota_t", [P, TILES], F32, p2)
        past = sb("past", [P, TILES * E], F32, p2)
        pastw = sb("pastw", [P, TILES * E], F32, p2)
        tile_e = sb("tile_e", [P, TILES], F32, p2)
        tile_r = sb("tile_r", [P, TILES], F32, p2)
        tab_e = sb("tab_e", [P, TILES], I32, p2)
        tab_r = sb("tab_r", [P, TILES], I32, p2)
        pad_f = sb("pad_f", [P, E], F32, p2)
        pad_i = sb("pad_i", [P, E], I32, p2)
        beyond = sb("beyond", [P, 2 * B * E], F32, p2)
        drop = sb("drop", [P, E], F32, p2)
        shift = sb("shift", [P, 2 * B], F32, p2)
        egap = sb("egap", [P, B], F32, p2)
        sden = sb("sden", [P, B], F32, p2)
        coef = [sb(f"coef{i}", [P, B], F32, p2) for i in range(2)]
        p2.close()

        bank = [top.enter_context(nc.psum_tensor(f"bank{i}", [P, 512], F32)) for i in range(8)]
        s_ps, st_ps, qt_ps, bank_a, bank_b = bank[0:2], bank[2:4], bank[4:6], bank[6], bank[7]

        const_ready = sem("const_ready")
        const_dma = sem("const_dma")
        gate_ready = sem("gate_ready")
        x_loaded = [sem(f"x_loaded{i}") for i in range(2)]
        c_loaded = [sem(f"c_loaded{i}") for i in range(2)]
        res_loaded = [sem(f"res_loaded{i}") for i in range(2)]
        w_loaded = sem("w_loaded")
        w_hi_done, w_lo_done = sem("w_hi_done"), sem("w_lo_done")
        n_stats, n_mv, n_ve, n_rs, n_done = (sem(f"n_{n}") for n in ("stats", "mv", "ve", "rs", "done"))
        q_hi, q_rem, q_mid, q_lo = (sem(f"q_{n}") for n in ("hi", "rem", "mid", "lo"))
        k_hi, k_rem_done, k_mid, k_lo, v_done = (sem(n) for n in ("k_hi", "k_rem_done", "k_mid", "k_lo", "v_done"))
        qt_done, qt_act, qt_dve = sem("qt_done"), sem("qt_act"), sem("qt_dve")
        s_done, max_done = sem("s_done"), sem("max_done")
        nm_hi, nm_remd, nm_mid, nm_lo = (sem(f"nm_{n}") for n in ("hi", "remd", "mid", "lo"))
        mt_done, mt_copied = sem("mt_done"), sem("mt_copied")
        mrow = [sem(f"mrow{i}") for i in range(2)]
        st_done, exp_done, pv_done, o_copied, on_done = (
            sem(n) for n in ("st_done", "exp_done", "pv_done", "o_copied", "on_done"))
        rden_done, att_done, res_done = (sem(n) for n in ("rden_done", "att_done", "res_done"))
        res_stored = [sem(f"res_stored{i}") for i in range(2)]
        o_stats, o_mv, o_ve, o_rs, z_done = (sem(n) for n in ("o_stats", "o_mv", "o_ve", "o_rs", "z_done"))
        zt_done, zt_copied, lg1_done, th_done, lg2_done, lg_copied = (
            sem(n) for n in ("zt_done", "zt_copied", "lg1_done", "th_done", "lg2_done", "lg_copied"))
        top_done, idx_done, idxf_done, masks_done, m12_done, gap_done = (
            sem(n) for n in ("top_done", "idx_done", "idxf_done", "masks_done", "m12_done", "gap_done"))
        rank_done, pos_done, run_done, slot_done, sloti_done, slotall_done = (
            sem(n) for n in ("rank_done", "pos_done", "run_done", "slot_done", "sloti_done", "slotall_done"))
        scattered = [sem(f"scattered{i}") for i in range(RING)]
        phase1_over, phase2_over = sem("phase1_over"), sem("phase2_over")
        bias_loaded, bias_done, dummy_done = sem("bias_loaded"), sem("bias_done"), sem("dummy_done")
        f_const, tab_step, tab_done, pad_idx, pads_done, exp2_done, coef_step = (
            sem(n) for n in ("f_const", "tab_step", "tab_done", "pad_idx", "pads_done", "exp2_done", "coef_step"))
        tile_loaded = [sem(f"tile_loaded{i}") for i in range(2)]
        ft_done, zh_done, zl_done, up_done, u_done, tanh_done, h_done = (
            sem(n) for n in ("ft_done", "zh_done", "zl_done", "up_done", "u_done", "tanh_done", "h_done"))
        ht_done, hh_done, hl_done, dn_done, y_done = (sem(n) for n in ("ht_done", "hh_done", "hl_done", "dn_done", "y_done"))
        y_stored = [sem(f"y_stored{i}") for i in range(2)]
        held = [sem(f"held{i}") for i in range(3)]
        gi_done = sem("gi_done")
        y1_loaded = [sem(f"y1_loaded{i}") for i in range(RING)]
        y2_loaded = [sem(f"y2_loaded{i}") for i in range(RING)]
        r_loaded = [sem(f"r_loaded{i}") for i in range(RING)]
        mix1, mix2 = sem("mix1"), sem("mix2")
        stored = [sem(f"stored{i}") for i in range(RING)]

        p3 = ExitStack()
        keep_coef = sb("over_phase2", [P, 2 * E * D // 4], F32, p3)
        p3.close()
        p3 = ExitStack()
        g_idx = [sb(f"g_idx{i}", [P, 2], I32, p3) for i in range(RING)]
        y1 = [sb(f"y1_{i}", [P, D], F32, p3) for i in range(RING)]
        y2 = [sb(f"y2_{i}", [P, D], F32, p3) for i in range(RING)]
        r_in = [sb(f"r_in{i}", [P, D], F32, p3) for i in range(RING)]
        p3.close()

        def expert_of(eng, t):
            return eng.value_load(tab_e[0:1, bass.ds(t, 1)], min_val=0, max_val=E - 1)

        block = top.enter_context(nc.Block())

        def ring2(b, p, per=16):
            return (b - p) * (per // 2) + per

        def ring4(b, q, per):
            return (b - q) * (per // 4) + per

        @block.sync
        def _(sp):
            sp.dma_start(gates_raw[:, 0:1], gx_d.rearrange("(a n) -> a n", a=1).to_broadcast([P, 1])).then_inc(const_dma, 16)
            sp.dma_start(gates_raw[:, 1:2], gf_d.rearrange("(a n) -> a n", a=1).to_broadcast([P, 1])).then_inc(const_dma, 16)
            sp.dma_start(wg1[:, :], wg1_d).then_inc(const_dma, 16)
            sp.dma_start(wg2[:, :], wg2_d).then_inc(const_dma, 16)

            def step(s, u):
                b, p = s - O_LOAD, (u - O_LOAD) % 2
                if valid(b):
                    wait(sp, q_lo, b - 1)
                    sp.dma_start(x_in[p][:, :], x_d[bass.ds(b, 1), :, :].rearrange("a s d -> (a s) d")).then_inc(x_loaded[p], 16)
                    wait(sp, k_hi, b - 1)
                    wait(sp, k_rem_done, b - 1)
                    wait(sp, v_done, b - 1)
                    sp.dma_start(c_in[p][:, :], ctx_d[bass.ds(b, 1), :, :].rearrange("a s d -> (a s) d")).then_inc(c_loaded[p], 16)
                    wait(sp, w_lo_done, b)
                    sp.dma_start(wst[:, :], w_d[bass.ds(b, 1), :, :].rearrange("a p n -> (a p) n")).then_inc(w_loaded, 16)
                b, p = s - O_ST, (u - O_ST) % 2
                if valid(b):
                    max_rows(b, p, 1)
                    wait(sp, z_done, b - 1)
                    wait(sp, res_stored[p], ring2(b - 2, p))
                    sp.dma_start(x_res[p][:, :], x_d[bass.ds(b, 1), :, :].rearrange("a s d -> (a s) d")).then_inc(res_loaded[p], 16)
                b, p = s - O_S, (u - O_S) % 2
                if valid(b):
                    max_rows(b, p, 0)
                b, p = s - O_OUT, (u - O_OUT) % 2
                if valid(b):
                    sp.wait_ge(res_done, b + 1)
                    sp.dma_start(x2_d[bass.ds(b, 1), :, :].rearrange("a s d -> (a s) d"), x_res[p][:, :]).then_inc(res_stored[p], 16)

            def max_rows(b, p, half):
                sp.wait_ge(mt_copied, 2 * b + half + 1)
                dst = kq[p][:, :].rearrange("r (m s) -> r m s", s=S)
                sp.dma_start(dst[QROWS:QROWS + MROWS, MHALF * half:MHALF * (half + 1), :],
                             mt_sb[half][:, :]).then_inc(mrow[half], 16)

            pipeline(sp, step, STEPS, LOOP0, B, RING)
            for p in range(2):
                sp.wait_ge(res_stored[p], ring2(B - 2 + p, p))
            sp.drain().then_inc(phase1_over, 1)
            sp.wait_ge(phase1_over, 5)

            sp.dma_start(bup[:, :], bup_d.to_broadcast([P, E * HE])).then_inc(bias_loaded, 16)
            sp.dma_start(bdn[:, :], bdn_d.to_broadcast([P, E * D])).then_inc(bias_loaded, 16)
            sp.wait_ge(f_const, 3)
            sp.dma_start(slots_d[E * REGION:ROWS, :].rearrange("(t p) d -> p t d", p=P),
                         zeros[:, :].unsqueeze(1).to_broadcast([P, DUMMY, D])).then_inc(dummy_done, 16)
            sp.wait_ge(dummy_done, 16)
            sp.wait_ge(pads_done, 16 * E)
            sp.wait_ge(tab_done, 2)

            def tile_step(s, u, fresh):
                t, p = s, u % 2
                if valid(t, TILES):
                    row = sp.value_load(tab_r[0:1, bass.ds(t, 1)], min_val=0, max_val=ROWS - P)
                    wait(sp, ft_done, t - 1)
                    sp.dma_start(z_s[p][:, :], slots_d[bass.ds(row, P), :]).then_inc(tile_loaded[p], 16)
                t, p = s - 4, u % 2
                if valid(t, TILES):
                    sp.wait_ge(y_done, t + 1)
                    sp.dma_start(y_d[bass.ds(t * P, P), :], y_sb[p][:, :]).then_inc(y_stored[p], 16)

            tile_pipeline(sp, tile_step)
            for p in range(2):
                last = TILES - 1 - (TILES - 1 - p) % 2
                sp.wait_ge(y_stored[p], ring2(last, p))
            sp.drain().then_inc(phase2_over, 1)
            sp.wait_ge(phase2_over, 5)

            def mix_step(s, q):
                b = s
                if valid(b):
                    wait(sp, stored[q], ring4(b - RING, q, 16))
                    sp.dma_start(r_in[q][:, :], x2_d[bass.ds(b, 1), :, :].rearrange("a s d -> (a s) d")).then_inc(r_loaded[q], 16)
                b, q = s - 3, (q - 3) % RING
                if valid(b):
                    sp.wait_ge(mix2, b + 1)
                    sp.dma_start(out_d[bass.ds(b, 1), :, :].rearrange("a s d -> (a s) d"), r_in[q][:, :]).then_inc(stored[q], 16)

            pipeline(sp, mix_step, B + 3, 8, B, RING)
            for q in range(RING):
                sp.wait_ge(stored[q], ring4(B - RING + q, q, 16))

        @block.gpsimd
        def _(pool):
            g = nc.gpsimd

            def hold(i, n):
                wait(pool, held[i], n)
                g.tensor_tensor(tock[:, i:i + 1], tick[:, :], tick[:, :], ALU.mult).then_inc(held[i], 1)

            g.memset(ident_f[:, :], 0.0).then_inc(const_ready, 1)
            g.memset(ident_b[:, :], 0.0).then_inc(const_ready, 1)
            g.memset(before[:, :], 0.0).then_inc(const_ready, 1)
            g.memset(ones_b[:, :], 1.0).then_inc(const_ready, 1)
            g.memset(minus_half[:, :], -0.5).then_inc(const_ready, 1)
            g.memset(eps[:, :], EPS).then_inc(const_ready, 1)
            g.memset(tick[:, :], 1.0).then_inc(const_ready, 1)
            for i in range(RING):
                g.memset(v_aug[i][:, :], 0.0).then_inc(const_ready, 1)
            for i in range(2):
                g.memset(nm_parts[i][:, :], 1.0).then_inc(const_ready, 1)
            g.iota(ebase[:, :], [[REGION, E]], base=0, channel_multiplier=0,
                   allow_small_or_imprecise_dtypes=True).then_inc(const_ready, 1)
            g.iota(run[:, :], [[REGION, E]], base=0, channel_multiplier=0,
                   allow_small_or_imprecise_dtypes=True).then_inc(const_ready, 1)
            g.iota(iota_e[:, :], [[1, E]], base=0, channel_multiplier=0,
                   allow_small_or_imprecise_dtypes=True).then_inc(const_ready, 1)
            g.iota(iota_p[:, :], [[1, 1]], base=0, channel_multiplier=1,
                   allow_small_or_imprecise_dtypes=True).then_inc(const_ready, 1)
            pool.wait_ge(const_ready, 17)
            for m in (ident_f, ident_b):
                g.affine_select(out=m[:, :], in_=m[:, :], compare_op=ALU.not_equal, fill=1.0, base=0,
                                pattern=[[-1, P]], channel_multiplier=1).then_inc(const_ready, 1)
            g.affine_select(out=before[:, :], in_=before[:, :], compare_op=ALU.is_ge, fill=1.0, base=0,
                            pattern=[[-1, P]], channel_multiplier=1).then_inc(const_ready, 1)
            last = g.memset(v_aug[0][:, :].rearrange("p (k c) -> p k c", c=32)[:, :, HD:HD + 1], 1.0)
            for i in range(1, RING):
                last = g.memset(v_aug[i][:, :].rearrange("p (k c) -> p k c", c=32)[:, :, HD:HD + 1], 1.0)
            last.then_inc(const_ready, 1)

            def step(s, u):
                b0 = s - O_LOAD
                b1, p1_ = s - O_NORM, (u - O_NORM) % 2
                b5, p5_, q5 = s - O_OUT, (u - O_OUT) % 2, (u - O_OUT) % RING
                b8, q8 = s - O_SLOT, (u - O_SLOT) % RING
                kn = k_nat[p1_][:, :].rearrange("p (k j d) -> p k j d", j=PARTS, d=HD)
                rem = k_rem[:, :].rearrange("p (k d) -> p k d", d=HD)
                qn = q_nat[p1_][:, :].rearrange("p (h j d) -> p h j d", j=4, d=HD)
                xv = x_in[p1_][:, :].rearrange("p (h d) -> p h d", d=HD)
                if valid(b1):
                    pool.wait_ge(w_hi_done, b1 + 1)
                    g.tensor_tensor(w_lo[:, bass.ds(b1 * WCHUNK, WCHUNK)], wst[:, :],
                                    w_hi[:, bass.ds(b1 * WCHUNK, WCHUNK)].bitcast(F32),
                                    ALU.subtract).then_inc(w_lo_done, 1)
                    pool.wait_ge(k_hi, b1 + 1)
                    g.tensor_tensor(rem, c_in[p1_][:, :].rearrange("p (k d) -> p k d", d=HD), kn[:, :, 3, :],
                                    ALU.subtract).then_inc(k_rem_done, 1)
                if valid(b8):
                    pool.wait_ge(sloti_done, b8 + 1)
                    hold(0, b8)
                    for j in range(2):
                        g.indirect_dma_start(
                            out=slots_d, out_offset=bass.IndirectOffsetOnAxis(ap=slot_i[q8][:, j:j + 1], axis=0),
                            in_=z[q8][:, :], in_offset=None).then_inc(scattered[q8], 16)
                if valid(b1):
                    pool.wait_ge(k_mid, b1 + 1)
                    g.tensor_tensor(kn[:, :, 0, :], rem, kn[:, :, 1, :], ALU.subtract).then_inc(k_lo, 1)
                    pool.wait_ge(q_hi, b1 + 1)
                    g.tensor_tensor(xv, xv, qn[:, :, 1, :], ALU.subtract).then_inc(q_rem, 1)
                if valid(b5):
                    pool.wait_ge(res_loaded[p5_], ring2(b5, p5_))
                    pool.wait_ge(att_done, 2 * b5 + 2)
                    g.tensor_tensor(x_res[p5_][:, :], x_res[p5_][:, :], z[q5][:, :], ALU.add).then_inc(res_done, 1)
                if valid(b1):
                    pool.wait_ge(q_mid, b1 + 1)
                    g.tensor_tensor(qn[:, :, 3, :], xv, qn[:, :, 2, :], ALU.subtract).then_inc(q_lo, 1)
                if valid(b0):
                    pool.wait_ge(n_mv, b0 + 1)
                    wait(pool, n_done, b0)
                    g.tensor_tensor(ve_n[:, :], mv_n[:, 1:2], eps[:, :], ALU.add).then_inc(n_ve, 1)
                    pool.wait_ge(n_ve, b0 + 1)
                    g.tensor_tensor(rs_n[:, :], ve_n[:, :], minus_half[:, :], ALU.pow).then_inc(n_rs, 1)
                if valid(b5):
                    pool.wait_ge(o_mv, b5 + 1)
                    g.tensor_tensor(ve_o[:, :], mv_o[:, 1:2], eps[:, :], ALU.add).then_inc(o_ve, 1)
                    pool.wait_ge(o_ve, b5 + 1)
                    g.tensor_tensor(rs_o[:, :], ve_o[:, :], minus_half[:, :], ALU.pow).then_inc(o_rs, 1)

            pipeline(pool, step, STEPS, LOOP0, B, RING)
            for q in range(RING):
                pool.wait_ge(scattered[q], ring4(B - RING + q, q, 32))
            pool.drain().then_inc(phase1_over, 1)
            pool.wait_ge(phase1_over, 5)

            g.iota(i128[:, :], [[P, B]], base=0, channel_multiplier=0,
                   allow_small_or_imprecise_dtypes=True).then_inc(f_const, 1)
            g.iota(iota_t[:, :], [[1, TILES]], base=0, channel_multiplier=0,
                   allow_small_or_imprecise_dtypes=True).then_inc(f_const, 1)
            g.memset(zeros[:, :], 0.0).then_inc(f_const, 1)
            pool.wait_ge(f_const, 3)
            pool.wait_ge(pad_idx, 2)
            for e in range(E):
                g.indirect_dma_start(out=slots_d, out_offset=bass.IndirectOffsetOnAxis(ap=pad_i[:, e:e + 1], axis=0),
                                     in_=zeros[:, :], in_offset=None).then_inc(pads_done, 16)
            pool.wait_ge(pads_done, 16 * E)
            pool.drain().then_inc(phase2_over, 1)
            pool.wait_ge(phase2_over, 5)

            def mix_step(s, q):
                b = s
                wait(pool, mix2, b - RING + 1)
                hold(1, b)
                g.tensor_copy(g_idx[q][:, :], rows_all[:, bass.ds(b * 2, 2)]).then_inc(gi_done, 1)
                pool.wait_ge(gi_done, b + 1)
                hold(2, b)
                for j, (y, done) in enumerate(((y1[q], y1_loaded[q]), (y2[q], y2_loaded[q]))):
                    g.indirect_dma_start(out=y[:, :], out_offset=None, in_=y_d,
                                         in_offset=bass.IndirectOffsetOnAxis(ap=g_idx[q][:, j:j + 1], axis=0)
                                         ).then_inc(done, 16)

            pipeline(pool, mix_step, B, 4, B, RING)

        @block.scalar
        def _(act):
            a = nc.scalar
            act.wait_ge(const_dma, 64)
            act.wait_ge(const_ready, 21)
            a.activation(gates[:, :], gates_raw[:, :], ACT.Tanh).then_inc(gate_ready, 1)
            act.wait_ge(gate_ready, 1)

            def step(s, u):
                b1, p1_, r1 = s - O_NORM, (u - O_NORM) % 2, (u - O_NORM) % RING
                b2, p2_ = s - O_QT, (u - O_QT) % 2
                b4 = s - O_ST
                b5 = s - O_OUT
                b6 = s - O_GATE
                for k in range(KV):
                    if valid(b4):
                        n = b4 * KV + k
                        act.wait_ge(st_done, n + 1)
                        if k == 0:
                            wait(act, pv_done, 2 * b4 - 1)
                        if k == 4:
                            wait(act, pv_done, 2 * b4)
                        a.activation(probs[:, k * G * S:(k + 1) * G * S], st_ps[k % 2][:, :], ACT.Exp,
                                     scale=HD ** -0.5).then_inc(exp_done, 1)
                    if k % 2 and valid(b2):
                        act.wait_ge(qt_done, b2 * KV + k + 1)
                        wait(act, st_done, (b2 - 2) * KV + k + 1)
                        a.activation(kq[p2_][0:QROWS, k * KQ:(k + 1) * KQ],
                                     qt_ps[k % 2][:, :].bitcast(BF16)[0:QROWS, 0:KQ], ACT.Copy).then_inc(qt_act, 1)
                    if k == 1 and valid(b5):
                        act.wait_ge(pv_done, 2 * b5 + 2)
                        act.wait_ge(on_done, 2 * b5 + 1)
                        a.activation(o_sb[:, :], bank_a[:, :], ACT.Copy).then_inc(o_copied, 1)
                    if k == 2 and valid(b6):
                        act.wait_ge(zt_done, b6 + 1)
                        wait(act, lg1_done, b6)
                        a.activation(z_t[:, :], bank_b[:, :], ACT.Copy).then_inc(zt_copied, 1)
                    if k == 0 and valid(b1):
                        act.wait_ge(c_loaded[p1_], ring2(b1, p1_))
                        wait(act, qt_done, (b1 - 1) * KV)
                        kn = k_nat[p1_][:, :].rearrange("p (k j d) -> p k j d", j=PARTS, d=HD)
                        a.activation(kn[:, :, 2:5, :], c_in[p1_][:, :].rearrange("p (k d) -> p k d", d=HD)
                                     .unsqueeze(2).to_broadcast([P, KV, 3, HD]), ACT.Copy).then_inc(k_hi, 1)
                    if k == 2 and valid(b1):
                        act.wait_ge(k_rem_done, b1 + 1)
                        a.activation(kn[:, :, 1:6:4, :], k_rem[:, :].rearrange("p (k d) -> p k d", d=HD)
                                     .unsqueeze(2).to_broadcast([P, KV, 2, HD]), ACT.Copy).then_inc(k_mid, 1)
                        wait(act, pv_done, 2 * (b1 - 3))
                        a.activation(v_aug[r1][:, :].rearrange("p (k c) -> p k c", c=32)[:, :, 0:HD],
                                     c_in[p1_][:, :].rearrange("p (k d) -> p k d", d=HD), ACT.Copy,
                                     scale=gates[:, 0:1]).then_inc(v_done, 1)
                    if k == 3 and valid(b1):
                        act.wait_ge(n_done, b1 + 1)
                        wait(act, qt_done, (b1 - 1) * KV)
                        qn = q_nat[p1_][:, :].rearrange("p (h j d) -> p h j d", j=4, d=HD)
                        a.activation(qn[:, :, 0:2, :], x_in[p1_][:, :].rearrange("p (h d) -> p h d", d=HD)
                                     .unsqueeze(2).to_broadcast([P, H, 2, HD]), ACT.Copy).then_inc(q_hi, 1)
                    if k == 4 and valid(b6):
                        act.wait_ge(lg1_done, b6 + 1)
                        wait(act, lg2_done, b6)
                        a.activation(th_sb[:, :], bank_a[0:E, 0:S], ACT.Tanh).then_inc(th_done, 1)
                    if k == 5 and valid(b4):
                        act.wait_ge(pv_done, 2 * b4 + 1)
                        wait(act, on_done, 2 * b4)
                        a.activation(o_sb[:, :], bank_a[:, :], ACT.Copy).then_inc(o_copied, 1)
                    if k == 6 and valid(b1):
                        act.wait_ge(q_rem, b1 + 1)
                        a.activation(qn[:, :, 2, :], x_in[p1_][:, :].rearrange("p (h d) -> p h d", d=HD),
                                     ACT.Copy).then_inc(q_mid, 1)
                    if k == 7 and valid(s):
                        act.wait_ge(w_loaded, 16 * (s + 1))
                        a.activation(w_hi[:, bass.ds(s * WCHUNK, WCHUNK)], wst[:, :], ACT.Copy).then_inc(w_hi_done, 1)

            pipeline(act, step, STEPS, LOOP0, B, RING)
            act.wait_ge(gap_done, B)
            act.drain().then_inc(phase1_over, 1)
            act.wait_ge(phase1_over, 5)
            a.activation(egap[:, :], gap_all[:, :], ACT.Exp).then_inc(exp2_done, 1)

            def tile_step(s, u, fresh):
                t, p = s - 3, (u - 3) % 2
                if valid(t, TILES):
                    act.wait_ge(ht_done, t + 1)
                    wait(act, dn_done, t - 1)
                    a.activation(hh[p][:, :], bank[4 + p][:, 0:HE], ACT.Copy).then_inc(hh_done, 1)
                t, p = s - 1, (u - 1) % 2
                if valid(t, TILES):
                    act.wait_ge(ft_done, t + 1)
                    wait(act, up_done, t - 1)
                    a.activation(zh[p][:, :], bank[p][:, :], ACT.Copy).then_inc(zh_done, 1)
                t, p = s - 2, (u - 2) % 2
                if valid(t, TILES):
                    act.wait_ge(u_done, t + 1)
                    wait(act, h_done, t - 1)
                    a.activation(t_sb[p][:, :], u_sb[p][:, :], ACT.Tanh, scale=0.5).then_inc(tanh_done, 1)

            tile_pipeline(act, tile_step)
            act.drain().then_inc(phase2_over, 1)

        @block.vector
        def _(dve):
            v = nc.vector
            dve.wait_ge(const_ready, 21)
            dve.wait_ge(gate_ready, 1)

            def max_part(b, p, half, n):
                src = nmax[p][:, H // 2 * half:H // 2 * (half + 1)].rearrange("p (k g) -> p k g", g=G)
                rem = nm_rem[half][:, :].rearrange("p (k g) -> p k g", g=G)
                hi, mid, lo = (nm_parts[half][:, MHALF * j:MHALF * (j + 1)]
                               .rearrange("p (k c) -> p k c", c=G + 1)[:, :, 1:] for j in range(MROWS))
                cnt = 2 * b + half + 1
                if n == 0:
                    wait(dve, mt_done, cnt - 2)
                    dve.wait_ge(max_done, KV * b + 4 * half + 4)
                    v.tensor_copy(hi, src).then_inc(nm_hi, 1)
                if n == 1:
                    dve.wait_ge(nm_hi, cnt)
                    v.tensor_tensor(rem, src, hi, ALU.subtract).then_inc(nm_remd, 1)
                if n == 2:
                    dve.wait_ge(nm_remd, cnt)
                    v.tensor_copy(mid, rem).then_inc(nm_mid, 1)
                if n == 3:
                    dve.wait_ge(nm_mid, cnt)
                    v.tensor_tensor(lo, rem, mid, ALU.subtract).then_inc(nm_lo, 1)

            def max_copy(b, half, src):
                dve.wait_ge(mt_done, 2 * b + half + 1)
                wait(dve, mrow[half], 16 * b)
                v.tensor_copy(mt_sb[half][:, :], src[:, :].bitcast(BF16)[0:MROWS * MHALF, 0:S]).then_inc(mt_copied, 1)

            def weights_sum(b, grp):
                o = bank_b[:, :].rearrange("p (g k c) -> p g k c", g=G, c=32)
                dve.wait_ge(on_done, 2 * b + grp + 1)
                v.reciprocal(rden[:, :].rearrange("p (g k) -> p g k", g=G), o[:, :, :, HD]).then_inc(rden_done, 1)

            def attend(b, q, grp):
                o = bank_b[:, :].rearrange("p (g k c) -> p g k c", g=G, c=32)
                dve.wait_ge(rden_done, 2 * b + grp + 1)
                if grp == 0:
                    wait(dve, scattered[q], ring4(b - RING, q, 32))
                v.tensor_tensor(
                    z[q][:, :].rearrange("p (k g d) -> p g k d", g=G, d=HD)[:, :, 4 * grp:4 * grp + 4, :],
                    o[:, :, :, 0:HD],
                    rden[:, :].rearrange("p (g k) -> p g k", g=G).unsqueeze(3).to_broadcast([P, G, 4, HD]),
                    ALU.mult).then_inc(att_done, 1)

            def step(s, u):
                b0, p0_ = s - O_LOAD, (u - O_LOAD) % 2
                b1, p1_ = s - O_NORM, (u - O_NORM) % 2
                b2, p2_ = s - O_QT, (u - O_QT) % 2
                b3, p3_ = s - O_S, (u - O_S) % 2
                b4 = s - O_ST
                b5, p5_, q5 = s - O_OUT, (u - O_OUT) % 2, (u - O_OUT) % RING
                b6, p6_, q6 = s - O_GATE, (u - O_GATE) % 2, (u - O_GATE) % RING
                b7, p7_ = s - O_ROUTE, (u - O_ROUTE) % 2
                b8, p8_, q8 = s - O_SLOT, (u - O_SLOT) % 2, (u - O_SLOT) % RING
                for k in range(KV):
                    if valid(b3):
                        n = b3 * KV + k
                        dve.wait_ge(s_done, n + 1)
                        v.tensor_reduce(nmax[p3_][:, k * G:(k + 1) * G],
                                        s_ps[k % 2][:, :].rearrange("p (g t) -> p g t", g=G),
                                        X_AXIS, ALU.max, negate=True).then_inc(max_done, 1)
                    if k % 2 == 0 and valid(b2):
                        dve.wait_ge(qt_done, b2 * KV + k + 1)
                        wait(dve, st_done, (b2 - 2) * KV + k + 1)
                        v.tensor_copy(kq[p2_][0:QROWS, k * KQ:(k + 1) * KQ],
                                      qt_ps[k % 2][:, :].bitcast(BF16)[0:QROWS, 0:KQ]).then_inc(qt_dve, 1)
                    if k == 0:
                        if valid(b7):
                            dve.wait_ge(lg_copied, b7 + 1)
                        if valid(b4):
                            max_copy(b4, 1, bank_a)
                        if valid(b6):
                            dve.wait_ge(o_rs, b6 + 1)
                            v.tensor_scalar(z[q6][:, :], x_res[p6_][:, :], mv_o[:, 0:1], rs_o[:, :], ALU.subtract,
                                            ALU.mult).then_inc(z_done, 1)
                        if valid(b7):
                            v.max(top8[:, :], lg_sb[p7_][:, :]).then_inc(top_done, 1)
                        if valid(b8):
                            dve.wait_ge(pos_done, b8 + 1)
                            v.tensor_tensor_reduce(out=junk[:, 0:E], in0=m1[p8_][:, :], in1=pos[:, :], scale=1.0,
                                                   scalar=0.0, op0=ALU.mult, op1=ALU.add,
                                                   accum_out=slot_f[:, 0:1]).then_inc(slot_done, 1)
                            v.tensor_tensor_reduce(out=junk[:, E:2 * E], in0=m2[p8_][:, :], in1=pos[:, :], scale=1.0,
                                                   scalar=0.0, op0=ALU.mult, op1=ALU.add,
                                                   accum_out=slot_f[:, 1:2]).then_inc(slot_done, 1)
                    if k == 1:
                        if valid(b5):
                            weights_sum(b5, 0)
                        if valid(b8):
                            dve.wait_ge(slot_done, 2 * b8 + 2)
                            v.tensor_copy(slot_i[q8][:, :], slot_f[:, :]).then_inc(sloti_done, 1)
                            v.tensor_copy(slot_all[:, bass.ds(b8 * 2, 2)], slot_f[:, :]).then_inc(slotall_done, 1)
                        if valid(b5):
                            attend(b5, q5, 0)
                        if valid(b7):
                            dve.wait_ge(top_done, b7 + 1)
                            v.tensor_tensor(gap_all[:, bass.ds(b7, 1)], top8[:, 1:2], top8[:, 0:1],
                                            ALU.subtract).then_inc(gap_done, 1)
                            v.max_index(idx8[:, :], top8[:, :], lg_sb[p7_][:, :]).then_inc(idx_done, 1)
                    if k == 2:
                        if valid(b1):
                            dve.wait_ge(n_rs, b1 + 1)
                            v.tensor_scalar(x_in[p1_][:, :], x_in[p1_][:, :], mv_n[:, 0:1], rs_n[:, :], ALU.subtract,
                                            ALU.mult).then_inc(n_done, 1)
                        if valid(b7):
                            dve.wait_ge(idx_done, b7 + 1)
                            v.tensor_copy(idxf[:, :], idx8[:, 0:2]).then_inc(idxf_done, 1)
                    if k == 3:
                        if valid(b3):
                            max_part(b3, p3_, 0, 0)
                        if valid(b7):
                            dve.wait_ge(idxf_done, b7 + 1)
                            v.tensor_scalar(m1[p7_][:, :], iota_e[:, :], idxf[:, 0:1], None,
                                            ALU.is_equal).then_inc(masks_done, 1)
                        if valid(b3):
                            max_part(b3, p3_, 0, 1)
                        if valid(b7):
                            v.tensor_scalar(m2[p7_][:, :], iota_e[:, :], idxf[:, 1:2], None,
                                            ALU.is_equal).then_inc(masks_done, 1)
                        if valid(b3):
                            max_part(b3, p3_, 0, 2)
                            max_part(b3, p3_, 0, 3)
                    if k == 4:
                        if valid(b5):
                            weights_sum(b5, 1)
                        if valid(b7):
                            dve.wait_ge(masks_done, 2 * b7 + 2)
                            v.tensor_tensor(m12[p7_][:, :], m1[p7_][:, :], m2[p7_][:, :], ALU.add).then_inc(m12_done, 1)
                        if valid(b5):
                            attend(b5, q5, 1)
                    if k == 5:
                        if valid(b0):
                            dve.wait_ge(x_loaded[p0_], ring2(b0, p0_))
                            v.bn_stats(st_n[:, :], x_in[p0_][:, :]).then_inc(n_stats, 1)
                        if valid(b3):
                            max_copy(b3, 0, bank_b)
                    if k == 6:
                        if valid(b5):
                            dve.wait_ge(res_done, b5 + 1)
                            v.bn_stats(st_o[:, :], x_res[p5_][:, :]).then_inc(o_stats, 1)
                        if valid(b0):
                            dve.wait_ge(n_stats, b0 + 1)
                            v.tensor_copy(junk[:, 2 * E + 2:2 * E + 4], st_n[:, 0:2])
                            v.bn_aggr(mv_n[:, :], st_n[:, :]).then_inc(n_mv, 1)
                    if k == 7:
                        if valid(b3):
                            max_part(b3, p3_, 1, 0)
                        if valid(b5):
                            dve.wait_ge(o_stats, b5 + 1)
                            v.tensor_copy(junk[:, 2 * E:2 * E + 2], st_o[:, 0:2])
                            v.bn_aggr(mv_o[:, :], st_o[:, :]).then_inc(o_mv, 1)
                        if valid(b3):
                            max_part(b3, p3_, 1, 1)
                        if valid(b7):
                            dve.wait_ge(rank_done, b7 + 1)
                            wait(dve, run_done, b7)
                            v.tensor_tensor(pos[:, :], bank_b[:, 0:E], run[:, :], ALU.add).then_inc(pos_done, 1)
                            v.tensor_tensor(run[:, :], run[:, :], bank_b[:, E:2 * E], ALU.add).then_inc(run_done, 1)
                        if valid(b3):
                            max_part(b3, p3_, 1, 2)
                        if valid(b6):
                            dve.wait_ge(lg2_done, b6 + 1)
                            v.tensor_copy(lg_sb[p6_][:, :], bank_a[:, 0:E]).then_inc(lg_copied, 1)
                        if valid(b3):
                            max_part(b3, p3_, 1, 3)

            pipeline(dve, step, STEPS, LOOP0, B, RING)
            dve.wait_ge(run_done, B)
            dve.drain().then_inc(phase1_over, 1)
            dve.wait_ge(phase1_over, 5)

            link = [0]

            def then(ins):
                link[0] += 1
                ins.then_inc(tab_step, 1)
                dve.wait_ge(tab_step, link[0])

            v.tensor_scalar(pad_f[:, :], run[:, :], iota_p[:, :], None, ALU.add).then_inc(pad_idx, 1)
            dve.wait_ge(pad_idx, 1)
            v.tensor_copy(pad_i[:, :], pad_f[:, :]).then_inc(pad_idx, 1)
            then(v.tensor_tensor(count[:, :], run[:, :], ebase[:, :], ALU.subtract))
            dve.wait_ge(f_const, 2)
            ov = over[:, :].rearrange("p (e i) -> p e i", e=E)
            then(v.tensor_tensor(ov, count[:, :].unsqueeze(2).to_broadcast([P, E, B]),
                                 i128[:, :].unsqueeze(1).to_broadcast([P, E, B]), ALU.is_gt))
            then(v.tensor_reduce(ntile[:, :], ov, X_AXIS, ALU.add))
            then(v.tensor_copy(tend[:, 0:1], ntile[:, 0:1]))
            for e in range(1, E):
                then(v.tensor_tensor(tend[:, e:e + 1], tend[:, e - 1:e], ntile[:, e:e + 1], ALU.add))
            then(v.tensor_scalar(tskip[:, :], ntile[:, :], float(-P), float(REGION), ALU.mult, ALU.add))
            pv_ = past[:, :].rearrange("p (t e) -> p t e", e=E)
            pw_ = pastw[:, :].rearrange("p (t e) -> p t e", e=E)
            then(v.tensor_tensor(pv_, iota_t[:, :].unsqueeze(2).to_broadcast([P, TILES, E]),
                                 tend[:, :].unsqueeze(1).to_broadcast([P, TILES, E]), ALU.is_ge))
            then(v.tensor_reduce(tile_e[:, :], pv_, X_AXIS, ALU.add))
            then(v.tensor_tensor(pw_, pv_, tskip[:, :].unsqueeze(1).to_broadcast([P, TILES, E]), ALU.mult))
            then(v.tensor_reduce(tile_r[:, :], pw_, X_AXIS, ALU.add))
            v.tensor_scalar(tab_e[:, :], tile_e[:, :], float(E - 1), None, ALU.min).then_inc(tab_done, 1)
            v.scalar_tensor_tensor(tab_r[:, :], iota_t[:, :], float(P), tile_r[:, :], ALU.mult,
                                   ALU.add).then_inc(tab_done, 1)
            then(v.tensor_scalar(drop[:, 0:1], tskip[:, 0:1], 0.0, None, ALU.mult))
            then(v.tensor_copy(drop[:, 1:E], tskip[:, 0:E - 1]))
            bv = beyond[:, :].rearrange("p (n e) -> p n e", e=E)
            then(v.tensor_tensor(bv, slot_all[:, :].unsqueeze(2).to_broadcast([P, 2 * B, E]),
                                 ebase[:, :].unsqueeze(1).to_broadcast([P, 2 * B, E]), ALU.is_ge))
            then(v.tensor_tensor(bv, bv, drop[:, :].unsqueeze(1).to_broadcast([P, 2 * B, E]), ALU.mult))
            then(v.tensor_reduce(shift[:, :], bv, X_AXIS, ALU.add))
            then(v.tensor_tensor(rows_all[:, :], slot_all[:, :], shift[:, :], ALU.subtract))
            dve.wait_ge(exp2_done, 1)
            then(v.tensor_scalar(sden[:, :], egap[:, :], 1.0, None, ALU.add))
            then(v.reciprocal(sden[:, :], sden[:, :]))
            then(v.tensor_scalar(coef[0][:, :], sden[:, :], gates[:, 1:2], 0.5, ALU.mult, ALU.mult))
            v.tensor_tensor(coef[1][:, :], coef[0][:, :], egap[:, :], ALU.mult).then_inc(coef_step, 1)
            dve.wait_ge(bias_loaded, 32)
            then(v.tensor_scalar(bdn[:, :], bdn[:, :], 2.0, None, ALU.mult))
            dve.wait_ge(tab_done, 2)

            expert = [None, None]

            def tile_step(s, u, fresh):
                expert[1] = expert[0]
                if valid(s - 2, TILES):
                    expert[0] = expert_of(dve, s - 2)
                t, p = s - 3, (u - 3) % 2
                if valid(t, TILES):
                    dve.wait_ge(hh_done, t + 1)
                    wait(dve, dn_done, t - 1)
                    v.tensor_tensor(hl[p][:, :], bank[4 + p][:, 0:HE], hh[p][:, :].bitcast(F32),
                                    ALU.subtract).then_inc(hl_done, 1)
                t, p = s - 1, (u - 1) % 2
                if valid(t, TILES):
                    dve.wait_ge(zh_done, t + 1)
                    wait(dve, up_done, t - 1)
                    v.tensor_tensor(zl[p][:, :], bank[p][:, :], zh[p][:, :].bitcast(F32),
                                    ALU.subtract).then_inc(zl_done, 1)
                t, p = s - 2, (u - 2) % 2
                if valid(t, TILES):
                    e = expert[0]
                    dve.wait_ge(up_done, t + 1)
                    wait(dve, tanh_done, t - 1)
                    v.tensor_tensor(u_sb[p][:, :], bank[2 + p][:, 0:HE], bup[:, bass.ds(e * HE, HE)],
                                    ALU.add).then_inc(u_done, 1)
                    dve.wait_ge(tanh_done, t + 1)
                    wait(dve, ht_done, t - 1)
                    v.scalar_tensor_tensor(h_sb[p][:, :], t_sb[p][:, :], 1.0, u_sb[p][:, :], ALU.add,
                                           ALU.mult).then_inc(h_done, 1)
                t, p = s - 3, (u - 3) % 2
                if valid(t, TILES):
                    e = expert_of(dve, t) if fresh else expert[1]
                    dve.wait_ge(dn_done, t + 1)
                    wait(dve, y_stored[p], ring2(t - 2, p))
                    v.tensor_tensor(y_sb[p][:, :], bank[6 + p][:, :], bdn[:, bass.ds(e * D, D)],
                                    ALU.add).then_inc(y_done, 1)

            tile_pipeline(dve, tile_step)
            dve.drain().then_inc(phase2_over, 1)

            def mix_step(s, q):
                b = s
                dve.wait_ge(r_loaded[q], ring4(b, q, 16))
                dve.wait_ge(y1_loaded[q], ring4(b, q, 16))
                v.scalar_tensor_tensor(r_in[q][:, :], y1[q][:, :], coef[0][:, bass.ds(b, 1)], r_in[q][:, :],
                                       ALU.mult, ALU.add).then_inc(mix1, 1)
                dve.wait_ge(mix1, b + 1)
                dve.wait_ge(y2_loaded[q], ring4(b, q, 16))
                v.scalar_tensor_tensor(r_in[q][:, :], y2[q][:, :], coef[1][:, bass.ds(b, 1)], r_in[q][:, :],
                                       ALU.mult, ALU.add).then_inc(mix2, 1)

            pipeline(dve, mix_step, B, 4, B, RING)

        @block.tensor
        def _(pe):
            t_ = nc.tensor
            pe.wait_ge(const_ready, 21)
            pe.wait_ge(const_dma, 64)

            def step(s, u):
                b2, p2_ = s - O_QT, (u - O_QT) % 2
                b3, p3_ = s - O_S, (u - O_S) % 2
                b4, p4_, r4 = s - O_ST, (u - O_ST) % 2, (u - O_ST) % RING
                b5, r5 = s - O_OUT, (u - O_OUT) % RING
                b6, q6 = s - O_GATE, (u - O_GATE) % RING
                b7, p7_ = s - O_ROUTE, (u - O_ROUTE) % 2
                b8 = s - O_SLOT

                def weighted_sum(b, r, grp):
                    for j in range(4):
                        k = 4 * grp + j
                        last = t_.matmul(bank_a[32 * j:32 * j + 32, :], v_aug[r][:, 32 * k:32 * k + 32],
                                         probs[:, k * G * S:(k + 1) * G * S], start=True, stop=True,
                                         tile_position=(0, 32 * j))
                    last.then_inc(pv_done, 1)

                def rows_back(b, grp):
                    pe.wait_ge(o_copied, 2 * b + grp + 1)
                    for g_ in range(G):
                        last = t_.transpose(bank_b[:, P * g_:P * g_ + P], o_sb[:, S * g_:S * g_ + S], ident_f[:, :])
                    last.then_inc(on_done, 1)

                def turn_maxima(b, half, dst):
                    pe.wait_ge(nm_lo, 2 * b + half + 1)
                    t_.transpose(dst[:, :].bitcast(BF16)[0:MWIDE, 0:S], nm_parts[half][:, :],
                                 ident_b[:, :]).then_inc(mt_done, 1)

                for k in range(KV):
                    if valid(b2):
                        if k == 0:
                            pe.wait_ge(q_lo, b2 + 1)
                            pe.wait_ge(k_lo, b2 + 1)
                        if k % 2 == 0:
                            wait(pe, qt_dve, b2 * 4 + k // 2)
                        else:
                            wait(pe, qt_act, b2 * 4 + k // 2)
                        dst = qt_ps[k % 2][:, :].bitcast(BF16)
                        t_.transpose(dst[0:QROWS, 0:P], k_nat[p2_][:, k * QROWS:(k + 1) * QROWS], ident_b[:, :])
                        for g_ in range(G):
                            h = k * G + g_
                            c0, cols = h * 4 * HD, slice(P + P * g_, 2 * P + P * g_)
                            t_.transpose(dst[0:4 * HD, cols], q_nat[p2_][:, c0:c0 + 4 * HD], ident_b[:, :])
                            last = t_.transpose(dst[4 * HD:QROWS, cols], q_nat[p2_][:, c0 + HD:c0 + 3 * HD],
                                                ident_b[:, :], tile_position=(0, 4 * HD))
                        last.then_inc(qt_done, 1)
                    if valid(b3):
                        if k % 2 == 0:
                            pe.wait_ge(qt_dve, b3 * 4 + k // 2 + 1)
                        else:
                            pe.wait_ge(qt_act, b3 * 4 + k // 2 + 1)
                        wait(pe, max_done, b3 * KV + (k - 1))
                        c = k * KQ
                        for g_ in range(G):
                            last = t_.matmul(s_ps[k % 2][:, P * g_:P * g_ + P],
                                             kq[p3_][0:QROWS, c + P + P * g_:c + 2 * P + P * g_],
                                             kq[p3_][0:QROWS, c:c + P], start=True, stop=True)
                        last.then_inc(s_done, 1)
                    if valid(b4):
                        if k % 4 == 0:
                            pe.wait_ge(mrow[k // 4], 16 * (b4 + 1))
                        wait(pe, exp_done, b4 * KV + (k - 1))
                        c = k * KQ
                        t_.matmul(st_ps[k % 2][:, :], kq[p4_][0:QROWS + MROWS, c:c + P],
                                  kq[p4_][0:QROWS + MROWS, c + P:c + KQ], start=True, stop=True).then_inc(st_done, 1)
                    if k == 0:
                        if valid(b5):
                            if valid(b8):
                                pe.wait_ge(run_done, b8 + 1)
                            elif valid(b4):
                                pe.wait_ge(mt_copied, 2 * b4 + 1)
                            rows_back(b5, 0)
                        if valid(b4):
                            if valid(b7):
                                pe.wait_ge(lg_copied, b7 + 1)
                            elif valid(b5):
                                pe.wait_ge(o_copied, 2 * b5 + 1)
                            turn_maxima(b4, 1, bank_a)
                    if k == 1 and valid(b5):
                        pe.wait_ge(exp_done, KV * b5 + KV)
                        if valid(b4):
                            pe.wait_ge(mt_copied, 2 * b4 + 2)
                        else:
                            pe.wait_ge(lg_copied, b7 + 1)
                        weighted_sum(b5, r5, 1)
                    if k == 2 and valid(b6):
                        pe.wait_ge(z_done, b6 + 1)
                        if valid(b5):
                            pe.wait_ge(att_done, 2 * b5 + 1)
                        else:
                            pe.wait_ge(run_done, b8 + 1)
                        for c in range(DC):
                            last = t_.transpose(bank_b[:, P * c:P * c + P], z[q6][:, P * c:P * c + P], ident_f[:, :])
                        last.then_inc(zt_done, 1)
                    if k == 3 and valid(b5):
                        if valid(b6):
                            pe.wait_ge(zt_copied, b6 + 1)
                        else:
                            pe.wait_ge(att_done, 2 * b5 + 1)
                        rows_back(b5, 1)
                    if k == 4 and valid(b6):
                        pe.wait_ge(zt_copied, b6 + 1)
                        if valid(b5):
                            pe.wait_ge(o_copied, 2 * b5 + 2)
                        else:
                            pe.wait_ge(lg_copied, b7 + 1)
                        for c in range(DC):
                            last = t_.matmul(bank_a[0:E, 0:S], wg1[:, c * E:(c + 1) * E], z_t[:, P * c:P * c + P],
                                             start=(c == 0), stop=(c == DC - 1))
                        last.then_inc(lg1_done, 1)
                    if k == 5 and valid(b4):
                        pe.wait_ge(exp_done, KV * b4 + 4)
                        pe.wait_ge(v_done, b4 + 1)
                        if valid(b6):
                            pe.wait_ge(th_done, b6 + 1)
                        elif valid(b5):
                            pe.wait_ge(o_copied, 2 * b5 + 2)
                        else:
                            pe.wait_ge(mt_copied, 2 * b4 + 2)
                        weighted_sum(b4, r4, 0)
                    if k == 5 and valid(b3):
                        if valid(b5):
                            pe.wait_ge(att_done, 2 * b5 + 2)
                        elif valid(b4):
                            wait(pe, mt_copied, 2 * b4 + 1)
                        turn_maxima(b3, 0, bank_b)
                    if k == 6:
                        if valid(b7):
                            pe.wait_ge(m12_done, b7 + 1)
                            if valid(b3):
                                pe.wait_ge(mt_copied, 2 * b3 + 1)
                            elif valid(b5):
                                pe.wait_ge(att_done, 2 * b5 + 2)
                            elif valid(b6):
                                pe.wait_ge(zt_copied, b6 + 1)
                            else:
                                pe.wait_ge(run_done, b7)
                            t_.matmul(bank_b[:, 0:E], before[:, :], m12[p7_][:, :], start=True, stop=True)
                            t_.matmul(bank_b[:, E:2 * E], ones_b[:, :], m12[p7_][:, :], start=True,
                                      stop=True).then_inc(rank_done, 1)
                    if k == 7:
                        if valid(b6):
                            pe.wait_ge(th_done, b6 + 1)
                            if valid(b4):
                                pe.wait_ge(o_copied, 2 * b4 + 1)
                            t_.matmul(bank_a[:, 0:E], th_sb[:, :], wg2[:, :], start=True, stop=True).then_inc(lg2_done, 1)

            pipeline(pe, step, STEPS, LOOP0, B, RING)
            pe.drain().then_inc(phase1_over, 1)
            pe.wait_ge(phase1_over, 5)
            pe.wait_ge(tab_done, 2)

            expert = [None, None]

            def tile_step(s, u, fresh):
                expert[1] = expert[0]
                if valid(s - 2, TILES):
                    expert[0] = expert_of(pe, s - 2)
                t, p = s - 1, (u - 1) % 2
                if valid(t, TILES):
                    wait(pe, zl_done, t - 1)
                    pe.wait_ge(tile_loaded[p], ring2(t, p))
                    for c in range(DC):
                        last = t_.transpose(bank[p][:, P * c:P * c + P], z_s[p][:, P * c:P * c + P], ident_f[:, :])
                    last.then_inc(ft_done, 1)
                t, p = s - 3, (u - 3) % 2
                if valid(t, TILES):
                    wait(pe, hl_done, t - 1)
                    pe.wait_ge(h_done, t + 1)
                    for c in range(HC):
                        last = t_.transpose(bank[4 + p][:, P * c:P * c + P], h_sb[p][:, P * c:P * c + P], ident_f[:, :])
                    last.then_inc(ht_done, 1)
                t, p = s - 2, (u - 2) % 2
                if valid(t, TILES):
                    wait(pe, u_done, t - 1)
                    pe.wait_ge(zl_done, t + 1)
                    o = bank[2 + p][:, 0:HE]
                    for c in range(DC):
                        cols = bass.ds(expert[0] * (DC * HE) + c * HE, HE)
                        t_.matmul(o, zh[p][:, P * c:P * c + P], w_hi[:, cols], start=(c == 0), stop=False)
                        t_.matmul(o, zh[p][:, P * c:P * c + P], w_lo[:, cols], start=False, stop=False)
                        last = t_.matmul(o, zl[p][:, P * c:P * c + P], w_hi[:, cols], start=False, stop=(c == DC - 1))
                    last.then_inc(up_done, 1)
                t, p = s - 3, (u - 3) % 2
                if valid(t, TILES):
                    if fresh:
                        expert[1] = expert_of(pe, t)
                    wait(pe, y_done, t - 1)
                    pe.wait_ge(hl_done, t + 1)
                    for c in range(HC):
                        cols = bass.ds(expert[1] * (HC * D) + (DOWN0 + c * D), D)
                        o = bank[6 + p][:, :]
                        t_.matmul(o, hh[p][:, P * c:P * c + P], w_hi[:, cols], start=(c == 0), stop=False)
                        t_.matmul(o, hh[p][:, P * c:P * c + P], w_lo[:, cols], start=False, stop=False)
                        last = t_.matmul(o, hl[p][:, P * c:P * c + P], w_hi[:, cols], start=False, stop=(c == HC - 1))
                    last.then_inc(dn_done, 1)

            tile_pipeline(pe, tile_step)
            pe.drain().then_inc(phase2_over, 1)


_INS = ["x", "ctx_512", "g_xattn", "g_ffn", "wg1", "wg2", "w", "bup", "bdn"]


def kernel(x, ctx_512, g_xattn, g_ffn, L0_ffn_Wg1, L0_ffn_Wg2, L0_ffn_Wup, L0_ffn_bup, L0_ffn_Wdown, L0_ffn_bdown):
    import numpy as np
    import concourse.bacc as bacc
    from concourse.bass_utils import run_bass_kernel_spmd

    wup, wdown = np.asarray(L0_ffn_Wup), np.asarray(L0_ffn_Wdown)
    up = wup.reshape(E, HE, DC, P).transpose(3, 0, 2, 1).reshape(P, DOWN0)
    down = wdown.reshape(E, D, HC, P).transpose(3, 0, 2, 1).reshape(P, WCOLS - DOWN0)
    w = np.concatenate([up, down], axis=1).reshape(P, WCOLS // WCHUNK, WCHUNK).transpose(1, 0, 2)
    data = {
        "x": x, "ctx_512": ctx_512, "g_xattn": g_xattn, "g_ffn": g_ffn,
        "wg1": np.asarray(L0_ffn_Wg1).reshape(E, DC, P).transpose(2, 1, 0).reshape(P, DC * E),
        "wg2": np.asarray(L0_ffn_Wg2).T,
        "w": w,
        "bup": np.asarray(L0_ffn_bup).reshape(1, E * HE),
        "bdn": np.asarray(L0_ffn_bdown).reshape(1, E * D),
    }
    nc = bacc.Bacc("TRN2", target_bir_lowering=False, num_devices=1)
    arrays, args = {}, []
    for name in _INS:
        a = np.ascontiguousarray(data[name])
        arrays[f"in_{name}"] = a
        args.append(nc.dram_tensor(f"in_{name}", a.shape, mybir.dt.from_np(a.dtype), kind="ExternalInput").ap())
    out = nc.dram_tensor("out", (B, S, D), F32, kind="ExternalOutput").ap()
    block_kernel(nc, *args, out)
    r = run_bass_kernel_spmd(nc, [arrays], core_ids=[0])
    return r.results[0]["out"]
```

```python
import concourse.bass as bass
from concourse import mybir
from contextlib import ExitStack

F32 = mybir.dt.float32
F32R = mybir.dt.float32r
BF16 = mybir.dt.bfloat16
I32 = mybir.dt.int32
U32 = mybir.dt.uint32
ALU = mybir.AluOpType
ACT = mybir.ActivationFunctionType
X_AXIS = mybir.AxisListType.X

P = 128
B, S, D = 32, 128, 512
KV, G, HD = 8, 4, 16
H = KV * G
E, HE = 8, 256
DC, HC = D // P, HE // P
PARTS = 6
QROWS = PARTS * HD
MROWS = 2
MHALF = KV // 2 * (G + 1)
MWIDE = 68
KQ = P + G * P
REGION = P + B * S
TILES = 2 * B * S // P + E - 1
ROWS = E * REGION
WCHUNK = 512
WCOLS = E * (DC * HE + HC * D)
DOWN0 = E * DC * HE
EPS = 1e-5
O_LOAD, O_NORM, O_QT, O_S, O_ST, O_OUT, O_GATE, O_ROUTE, O_SLOT = range(9)
STEPS = B + O_SLOT
LOOP0 = 12
MIXLAG = 4
MIXRING = 8
TURN_DVE = (0, 2, 4)
RING = 4


def valid(b, n=B):
    return not isinstance(b, int) or 0 <= b < n


def turned(k, b):
    on_dve = k in TURN_DVE
    mine = [j for j in range(KV) if (j in TURN_DVE) == on_dve]
    return on_dve, b * len(mine) + mine.index(k) + 1


def wait(eng, sem, value):
    if not isinstance(value, int) or value > 0:
        eng.wait_ge(sem, value)


def pipeline(eng, step, steps, first, last, unroll):
    for s in range(first):
        step(s, s % unroll)
    with eng.Fori(0, (last - first) // unroll) as i:
        for u in range(unroll):
            step(i * unroll + (first + u), (first + u) % unroll)
    for s in range(last, steps):
        step(s, s % unroll)


def tile_pipeline(eng, step):
    first, unroll = 8, 16
    last = first + (TILES - first) // unroll * unroll
    for s in range(first):
        step(s, s % unroll, s == 0)
    with eng.Fori(0, (last - first) // unroll) as i:
        for u in range(unroll):
            step(i * unroll + (first + u), u, u == 0)
    for s in range(last, TILES + 4):
        step(s, s % unroll, s == last)


def block_kernel(nc, x_d, ctx_d, gx_d, gf_d, wg1_d, wg2_d, w_d, bup_d, bdn_d, out_d):
    slots_d = nc.dram_tensor("slots", (ROWS, D), F32, kind="Internal").ap()
    y_d = nc.dram_tensor("expert_out", (TILES * P, D), F32, kind="Internal").ap()
    x2_d = nc.dram_tensor("x2_scratch", (B, S, D), F32, kind="Internal").ap()

    top = ExitStack()
    with top:
        def sb(name, shape, dt, stack=top):
            return stack.enter_context(nc.sbuf_tensor(name, shape, dt))

        def sem(name):
            return top.enter_context(nc.semaphore(name))

        slot_all = sb("slot_all", [P, 2 * B], F32)
        gap_all = sb("gap_all", [P, B], F32)
        run = sb("run", [P, E], F32)
        ebase = sb("ebase", [P, E], F32)
        tick = sb("tick", [P, 1], F32)
        tock = sb("tock", [P, 3], F32)
        ident_f = sb("ident_f", [P, P], F32)
        iota_t = sb("iota_t", [P, TILES], F32)
        e_diff = sb("e_diff", [P, E * E], F32)
        gates = sb("gates", [P, 2], F32)
        gates_raw = sb("gates_raw", [P, 2], F32)

        p12 = ExitStack()
        w_hi = sb("w_hi", [P, WCOLS], F32R, p12)
        w_lo = sb("w_lo", [P, WCOLS], F32R, p12)

        p1 = ExitStack()
        z = [sb(f"z{i}", [P, D], F32, p1) for i in range(RING)]
        slot_i = [sb(f"slot_i{i}", [P, 2], I32, p1) for i in range(RING)]
        wst = sb("wst", [P, WCHUNK], F32, p1)
        x_in = [sb(f"x_in{i}", [P, D], F32, p1) for i in range(2)]
        c_in = [sb(f"c_in{i}", [P, P], F32, p1) for i in range(2)]
        q_nat = [sb(f"q_nat{i}", [P, H * 4 * HD], BF16, p1) for i in range(2)]
        k_nat = [sb(f"k_nat{i}", [P, KV * QROWS], BF16, p1) for i in range(2)]
        k_rem = sb("k_rem", [P, P], F32, p1)
        v_aug = [sb(f"v_aug{i}", [P, KV * 32], F32, p1) for i in range(RING)]
        kq = [sb(f"kq{i}", [P, KV * KQ], BF16, p1) for i in range(2)]
        probs = sb("probs", [P, KV * G * S], F32, p1)
        o_sb = sb("o_sb", [P, G * S], F32, p1)
        x_res = [sb(f"x_res{i}", [P, D], F32, p1) for i in range(2)]
        z_t = sb("z_t", [P, D], F32, p1)
        nmax = [sb(f"nmax{i}", [P, H], F32, p1) for i in range(2)]
        nm_parts = [sb(f"nm_parts{i}", [P, MWIDE], BF16, p1) for i in range(2)]
        mt_sb = [sb(f"mt_sb{i}", [MROWS * MHALF, S], BF16, p1) for i in range(2)]
        ident_b = sb("ident_b", [P, P], BF16, p1)
        before = sb("before", [P, P], BF16, p1)
        ones_b = sb("ones_b", [P, P], BF16, p1)
        wg1 = sb("wg1", [P, DC * E], F32, p1)
        wg2 = sb("wg2", [E, E], F32, p1)
        st_n = sb("st_n", [P, 6], F32, p1)
        mv_n = sb("mv_n", [P, 2], F32, p1)
        ve_n = sb("ve_n", [P, 1], F32, p1)
        rs_n = sb("rs_n", [P, 1], F32, p1)
        st_o = sb("st_o", [P, 6], F32, p1)
        mv_o = sb("mv_o", [P, 2], F32, p1)
        ve_o = sb("ve_o", [P, 1], F32, p1)
        rs_o = sb("rs_o", [P, 1], F32, p1)
        minus_half = sb("minus_half", [P, 1], F32, p1)
        eps = sb("eps", [P, 1], F32, p1)
        rden = sb("rden", [P, G * 4], F32, p1)
        th_sb = sb("th_sb", [E, S], F32, p1)
        lg_sb = [sb(f"lg_sb{i}", [P, E], F32, p1) for i in range(2)]
        top8 = sb("top8", [P, E], F32, p1)
        idx8 = sb("idx8", [P, E], U32, p1)
        idxf = sb("idxf", [P, 2], F32, p1)
        m1 = [sb(f"m1_{i}", [P, E], F32, p1) for i in range(2)]
        m2 = [sb(f"m2_{i}", [P, E], F32, p1) for i in range(2)]
        m12 = [sb(f"m12_{i}", [P, E], BF16, p1) for i in range(2)]
        pos = sb("pos", [P, E], F32, p1)
        junk = sb("junk", [P, 3 * E], F32, p1)
        slot_f = sb("slot_f", [P, 2], F32, p1)
        p1.close()

        p23 = ExitStack()
        r_in = [sb(f"r_in{i}", [P, D], F32, p23) for i in range(MIXRING)]
        coef = [sb(f"coef{i}", [P, B], F32, p23) for i in range(2)]
        rows_all = sb("rows_all", [P, 2 * B], I32, p23)

        p2 = ExitStack()
        bup = sb("bup", [P, E * HE], F32, p2)
        bdn = sb("bdn", [P, E * D], F32, p2)             
        z_s = [sb(f"z_s{i}", [P, D], F32, p2) for i in range(RING)]
        zh = [sb(f"zh{i}", [P, D], F32R, p2) for i in range(2)]
        zl = [sb(f"zl{i}", [P, D], F32R, p2) for i in range(2)]
        u_sb = [sb(f"u_sb{i}", [P, HE], F32, p2) for i in range(2)]
        t_sb = [sb(f"t_sb{i}", [P, HE], F32, p2) for i in range(2)]
        h_sb = [sb(f"h_sb{i}", [P, HE], F32, p2) for i in range(2)]
        hh = [sb(f"hh{i}", [P, HE], F32R, p2) for i in range(2)]
        hl = [sb(f"hl{i}", [P, HE], F32R, p2) for i in range(2)]
        y_sb = [sb(f"y_sb{i}", [P, D], F32, p2) for i in range(2)]
        count = sb("count", [P, E], F32, p2)
        ntile = sb("ntile", [P, E], F32, p2)
        tend = sb("tend", [P, E], F32, p2)
        row0 = sb("row0", [P, E], F32, p2)
        past = sb("past", [P, TILES * E], F32, p2)
        pastw = sb("pastw", [P, TILES * E], F32, p2)
        tile_e = sb("tile_e", [P, TILES], F32, p2)
        tile_r = sb("tile_r", [P, TILES], F32, p2)
        tab_e = sb("tab_e", [P, TILES], I32, p2)
        tab_r = sb("tab_r", [P, TILES], I32, p2)
        upto = sb("upto", [P, E * E], F32, p2)
        upton = sb("upton", [P, E * E], F32, p2)
        live = sb("live", [P, TILES], F32, p2)
        row_f = sb("row_f", [P, TILES], F32, p2)
        drop = sb("drop", [P, E + 1], F32, p2)
        shift = sb("shift", [P, 2 * B], F32, p2)
        egap = sb("egap", [P, B], F32, p2)
        sden = sb("sden", [P, B], F32, p2)
        p2.close()

        p23.close()
        p12.close()

        p3 = ExitStack()
        r_late = sb("r_late", [P, (B - MIXRING) * D], F32, p3)
        g_idx = [sb(f"g_idx{i}", [P, 2], I32, p3) for i in range(MIXRING)]
        y1 = [sb(f"y1_{i}", [P, D], F32, p3) for i in range(MIXRING)]
        y2 = [sb(f"y2_{i}", [P, D], F32, p3) for i in range(MIXRING)]
        p3.close()

        bank = [top.enter_context(nc.psum_tensor(f"bank{i}", [P, 512], F32)) for i in range(8)]
        s_ps, st_ps, qt_ps, bank_a, bank_b = bank[0:2], bank[2:4], bank[4:6], bank[6], bank[7]

        const_ready = sem("const_ready")
        const_dma = sem("const_dma")
        gate_ready = sem("gate_ready")
        x_loaded = [sem(f"x_loaded{i}") for i in range(2)]
        c_loaded = [sem(f"c_loaded{i}") for i in range(2)]
        res_loaded = [sem(f"res_loaded{i}") for i in range(2)]
        w_loaded = sem("w_loaded")
        w_hi_done, w_lo_done = sem("w_hi_done"), sem("w_lo_done")
        n_stats, n_mv, n_ve, n_rs, n_done = (sem(f"n_{n}") for n in ("stats", "mv", "ve", "rs", "done"))
        q_hi, q_rem, q_mid, q_lo = (sem(f"q_{n}") for n in ("hi", "rem", "mid", "lo"))
        k_hi, k_rem_done, k_mid, k_lo, v_done = (sem(n) for n in ("k_hi", "k_rem_done", "k_mid", "k_lo", "v_done"))
        qt_done, qt_act, qt_dve = sem("qt_done"), sem("qt_act"), sem("qt_dve")
        s_done, max_done = sem("s_done"), sem("max_done")
        nm_hi, nm_lo = sem("nm_hi"), sem("nm_lo")
        mt_done, mt_copied = sem("mt_done"), sem("mt_copied")
        mrow = [sem(f"mrow{i}") for i in range(2)]
        st_done, exp_done, pv_done, o_copied, on_done = (
            sem(n) for n in ("st_done", "exp_done", "pv_done", "o_copied", "on_done"))
        rden_done, att_done, res_done = (sem(n) for n in ("rden_done", "att_done", "res_done"))
        res_stored = [sem(f"res_stored{i}") for i in range(2)]
        o_stats, o_mv, o_ve, o_rs, z_done = (sem(n) for n in ("o_stats", "o_mv", "o_ve", "o_rs", "z_done"))
        zt_done, zt_copied, lg1_done, th_done, lg2_done, lg_copied = (
            sem(n) for n in ("zt_done", "zt_copied", "lg1_done", "th_done", "lg2_done", "lg_copied"))
        top_done, idx_done, idxf_done, masks_done, m12_done, gap_done = (
            sem(n) for n in ("top_done", "idx_done", "idxf_done", "masks_done", "m12_done", "gap_done"))
        rank_done, pos_done, run_done, slot_done, sloti_done, slotall_done = (
            sem(n) for n in ("rank_done", "pos_done", "run_done", "slot_done", "sloti_done", "slotall_done"))
        scattered = [sem(f"scattered{i}") for i in range(RING)]
        phase1_over, phase2_over = sem("phase1_over"), sem("phase2_over")
        bup_loaded, bdn_loaded, scatter_over = sem("bup_loaded"), sem("bdn_loaded"), sem("scatter_over")
        tab_step, tab_done, pads_done, exp2_done, coef_step = (
            sem(n) for n in ("tab_step", "tab_done", "pads_done", "exp2_done", "coef_step"))
        tile_loaded = [sem(f"tile_loaded{i}") for i in range(RING)]
        ft_done, zh_done, zl_done, up_done, u_done, tanh_done, h_done = (
            sem(n) for n in ("ft_done", "zh_done", "zl_done", "up_done", "u_done", "tanh_done", "h_done"))
        ht_done, hh_done, hl_done, dn_done, y_done = (sem(n) for n in ("ht_done", "hh_done", "hl_done", "dn_done", "y_done"))
        y_stored = [sem(f"y_stored{i}") for i in range(2)]
        held = [sem(f"held{i}") for i in range(3)]
        gi_done = sem("gi_done")
        y1_loaded = [sem(f"y1_loaded{i}") for i in range(MIXRING)]
        y2_loaded = [sem(f"y2_loaded{i}") for i in range(MIXRING)]
        r_loaded = [sem(f"r_loaded{i}") for i in range(MIXRING)]
        mix1, mix2 = sem("mix1"), sem("mix2")
        stored = [sem(f"stored{i}") for i in range(MIXRING)]

        def expert_of(eng, t):
            return eng.value_load(tab_e[0:1, bass.ds(t, 1)], min_val=0, max_val=E - 1)

        block = top.enter_context(nc.Block())

        def ring2(b, p, per=16):
            return (b - p) * (per // 2) + per

        def ring4(b, q, per):
            return (b - q) * (per // 4) + per

        def mixed(b, q):
            return (b - q) * (16 // MIXRING) + 16

        def residual(b):
            if isinstance(b, int) and b < MIXRING:
                return r_in[b][:, :]
            return r_late[:, bass.ds(b * D - MIXRING * D, D)]

        @block.sync
        def _(sp):
            def step(s, u):
                b, p = s - O_LOAD, (u - O_LOAD) % 2
                if valid(b):
                    wait(sp, q_lo, b - 1)
                    sp.dma_start(x_in[p][:, :], x_d[bass.ds(b, 1), :, :].rearrange("a s d -> (a s) d")).then_inc(x_loaded[p], 16)
                    wait(sp, k_hi, b - 1)
                    wait(sp, k_rem_done, b - 1)
                    wait(sp, v_done, b - 1)
                    sp.dma_start(c_in[p][:, :], ctx_d[bass.ds(b, 1), :, :].rearrange("a s d -> (a s) d")).then_inc(c_loaded[p], 16)
                    wait(sp, w_lo_done, b)
                    sp.dma_start(wst[:, :], w_d[bass.ds(b, 1), :, :].rearrange("a p n -> (a p) n")).then_inc(w_loaded, 16)
                b, p = s - O_ST, (u - O_ST) % 2
                if valid(b):
                    max_rows(b, p, 1)
                    wait(sp, z_done, b - 1)
                    wait(sp, res_stored[p], ring2(b - 2, p))
                    sp.dma_start(x_res[p][:, :], x_d[bass.ds(b, 1), :, :].rearrange("a s d -> (a s) d")).then_inc(res_loaded[p], 16)
                b, p = s - O_S, (u - O_S) % 2
                if valid(b):
                    max_rows(b, p, 0)
                b, p = s - O_OUT, (u - O_OUT) % 2
                if isinstance(s, int) and s == 2:
                    sp.wait_ge(const_ready, 22)
                    sp.dma_start(slots_d.rearrange("(e r) d -> r e d", e=E)[0:P, :, :],
                                 z_t[:, :].unsqueeze(1).to_broadcast([P, E, D])).then_inc(pads_done, 16)
                if valid(b):
                    sp.wait_ge(res_done, b + 1)
                    sp.dma_start(x2_d[bass.ds(b, 1), :, :].rearrange("a s d -> (a s) d"), x_res[p][:, :]).then_inc(res_stored[p], 16)

            def max_rows(b, p, half):
                sp.wait_ge(mt_copied, 2 * b + half + 1)
                dst = kq[p][:, :].rearrange("r (m s) -> r m s", s=S)
                sp.dma_start(dst[QROWS:QROWS + MROWS, MHALF * half:MHALF * (half + 1), :],
                             mt_sb[half][:, :]).then_inc(mrow[half], 16)

            pipeline(sp, step, STEPS, LOOP0, B, RING)
            for p in range(2):
                sp.wait_ge(res_stored[p], ring2(B - 2 + p, p))
            sp.drain().then_inc(phase1_over, 1)
            sp.wait_ge(phase1_over, 4)

            sp.wait_ge(scatter_over, 1)
            sp.wait_ge(pads_done, 16)
            sp.wait_ge(tab_done, 1)

            def tile_step(s, u, fresh):
                t, r = s, u % RING
                if valid(t, TILES):
                    row = sp.value_load(tab_r[0:1, bass.ds(t, 1)], min_val=0, max_val=ROWS - P)
                    wait(sp, ft_done, t - RING + 1)
                    sp.dma_start(z_s[r][:, :], slots_d[bass.ds(row, P), :]).then_inc(tile_loaded[r], 16)
                    if isinstance(t, int) and t == 1:
                        sp.dma_start(bup[:, :], bup_d.to_broadcast([P, E * HE])).then_inc(bup_loaded, 16)
                    if isinstance(t, int) and t == 3:
                        sp.dma_start(bdn[:, :], bdn_d.to_broadcast([P, E * D])).then_inc(bdn_loaded, 16)
                q = s - (TILES + 4 - MIXRING)
                if isinstance(s, int) and q >= 0:
                    load_residual(q, q)
                t, p = s - 4, u % 2
                if valid(t, TILES):
                    sp.wait_ge(y_done, t + 1)
                    sp.dma_start(y_d[bass.ds(t * P, P), :], y_sb[p][:, :]).then_inc(y_stored[p], 16)

            def load_residual(b, q):
                sp.dma_start(residual(b), x2_d[bass.ds(b, 1), :, :].rearrange("a s d -> (a s) d")).then_inc(r_loaded[q], 16)

            tile_pipeline(sp, tile_step)
            for p in range(2):
                last = TILES - 1 - (TILES - 1 - p) % 2
                sp.wait_ge(y_stored[p], ring2(last, p))
            sp.drain().then_inc(phase2_over, 1)
            sp.wait_ge(phase2_over, 5)

            def mix_step(s, q):
                b = s + MIXRING
                if valid(b):
                    sp.wait_ge(r_loaded[q], mixed(s, q))
                    load_residual(b, q)
                b, q = s - MIXLAG, (q - MIXLAG) % MIXRING
                if valid(b):
                    sp.wait_ge(mix2, b + 1)
                    sp.dma_start(out_d[bass.ds(b, 1), :, :].rearrange("a s d -> (a s) d"), residual(b)).then_inc(stored[q], 16)

            pipeline(sp, mix_step, B + MIXLAG, 2 * MIXRING, B - MIXRING, MIXRING)
            for q in range(MIXRING):
                sp.wait_ge(stored[q], mixed(B - MIXRING + q, q))

        @block.gpsimd
        def _(pool):
            g = nc.gpsimd

            def hold(i, n):
                wait(pool, held[i], n)
                g.tensor_tensor(tock[:, i:i + 1], tick[:, :], tick[:, :], ALU.mult).then_inc(held[i], 1)

            g.memset(ident_f[:, :], 0.0).then_inc(const_ready, 1)
            g.memset(ident_b[:, :], 0.0).then_inc(const_ready, 1)
            g.memset(before[:, :], 0.0).then_inc(const_ready, 1)
            g.memset(ones_b[:, :], 1.0).then_inc(const_ready, 1)
            g.memset(minus_half[:, :], -0.5).then_inc(const_ready, 1)
            g.memset(eps[:, :], EPS).then_inc(const_ready, 1)
            g.memset(tick[:, :], 1.0).then_inc(const_ready, 1)
            g.memset(z_t[:, :], 0.0).then_inc(const_ready, 1)
            for i in range(RING):
                g.memset(v_aug[i][:, :], 0.0).then_inc(const_ready, 1)
            for i in range(2):
                g.memset(nm_parts[i][:, :], 1.0).then_inc(const_ready, 1)
            g.iota(ebase[:, :], [[REGION, E]], base=P, channel_multiplier=0,
                   allow_small_or_imprecise_dtypes=True).then_inc(const_ready, 1)
            g.iota(run[:, :], [[REGION, E]], base=P, channel_multiplier=0,
                   allow_small_or_imprecise_dtypes=True).then_inc(const_ready, 1)
            g.iota(iota_t[:, :], [[1, TILES]], base=0, channel_multiplier=0,
                   allow_small_or_imprecise_dtypes=True).then_inc(const_ready, 1)
            g.iota(e_diff[:, :], [[-1, E], [1, E]], base=0, channel_multiplier=0,
                   allow_small_or_imprecise_dtypes=True).then_inc(const_ready, 1)
            pool.wait_ge(const_ready, 18)
            for m in (ident_f, ident_b):
                g.affine_select(out=m[:, :], in_=m[:, :], compare_op=ALU.not_equal, fill=1.0, base=0,
                                pattern=[[-1, P]], channel_multiplier=1).then_inc(const_ready, 1)
            g.affine_select(out=before[:, :], in_=before[:, :], compare_op=ALU.is_ge, fill=1.0, base=0,
                            pattern=[[-1, P]], channel_multiplier=1).then_inc(const_ready, 1)
            last = g.memset(v_aug[0][:, :].rearrange("p (k c) -> p k c", c=32)[:, :, HD:HD + 1], 1.0)
            for i in range(1, RING):
                last = g.memset(v_aug[i][:, :].rearrange("p (k c) -> p k c", c=32)[:, :, HD:HD + 1], 1.0)
            last.then_inc(const_ready, 1)

            def step(s, u):
                b0 = s - O_LOAD
                b1, p1_ = s - O_NORM, (u - O_NORM) % 2
                b5, p5_, q5 = s - O_OUT, (u - O_OUT) % 2, (u - O_OUT) % RING
                b8, q8 = s - O_SLOT, (u - O_SLOT) % RING
                kn = k_nat[p1_][:, :].rearrange("p (k j d) -> p k j d", j=PARTS, d=HD)
                rem = k_rem[:, :].rearrange("p (k d) -> p k d", d=HD)
                qn = q_nat[p1_][:, :].rearrange("p (h j d) -> p h j d", j=4, d=HD)
                xv = x_in[p1_][:, :].rearrange("p (h d) -> p h d", d=HD)
                if valid(b1):
                    pool.wait_ge(w_hi_done, b1 + 1)
                    g.tensor_tensor(w_lo[:, bass.ds(b1 * WCHUNK, WCHUNK)], wst[:, :],
                                    w_hi[:, bass.ds(b1 * WCHUNK, WCHUNK)].bitcast(F32),
                                    ALU.subtract).then_inc(w_lo_done, 1)
                    pool.wait_ge(k_hi, b1 + 1)
                    g.tensor_tensor(rem, c_in[p1_][:, :].rearrange("p (k d) -> p k d", d=HD), kn[:, :, 3, :],
                                    ALU.subtract).then_inc(k_rem_done, 1)
                    pool.wait_ge(k_rem_done, b1 + 1)
                    g.tensor_tensor(kn[:, :, 1:6:4, :], rem.unsqueeze(2).to_broadcast([P, KV, 2, HD]),
                                    tick[:, :].unsqueeze(2).unsqueeze(3).to_broadcast([P, KV, 2, HD]),
                                    ALU.mult).then_inc(k_mid, 1)
                if valid(b8):
                    pool.wait_ge(sloti_done, b8 + 1)
                    hold(0, b8)
                    for j in range(2):
                        g.indirect_dma_start(
                            out=slots_d, out_offset=bass.IndirectOffsetOnAxis(ap=slot_i[q8][:, j:j + 1], axis=0),
                            in_=z[q8][:, :], in_offset=None).then_inc(scattered[q8], 16)
                if valid(b1):
                    pool.wait_ge(k_mid, b1 + 1)
                    g.tensor_tensor(kn[:, :, 0, :], rem, kn[:, :, 1, :], ALU.subtract).then_inc(k_lo, 1)
                    pool.wait_ge(q_hi, b1 + 1)
                    g.tensor_tensor(xv, xv, qn[:, :, 1, :], ALU.subtract).then_inc(q_rem, 1)
                if valid(b5):
                    pool.wait_ge(res_loaded[p5_], ring2(b5, p5_))
                    pool.wait_ge(att_done, 2 * b5 + 2)
                    g.tensor_tensor(x_res[p5_][:, :], x_res[p5_][:, :], z[q5][:, :], ALU.add).then_inc(res_done, 1)
                if valid(b1):
                    pool.wait_ge(q_mid, b1 + 1)
                    g.tensor_tensor(qn[:, :, 3, :], xv, qn[:, :, 2, :], ALU.subtract).then_inc(q_lo, 1)
                if valid(b0):
                    pool.wait_ge(n_mv, b0 + 1)
                    wait(pool, n_done, b0)
                    g.tensor_tensor(ve_n[:, :], mv_n[:, 1:2], eps[:, :], ALU.add).then_inc(n_ve, 1)
                    pool.wait_ge(n_ve, b0 + 1)
                    g.tensor_tensor(rs_n[:, :], ve_n[:, :], minus_half[:, :], ALU.pow).then_inc(n_rs, 1)
                if valid(b5):
                    pool.wait_ge(o_mv, b5 + 1)
                    g.tensor_tensor(ve_o[:, :], mv_o[:, 1:2], eps[:, :], ALU.add).then_inc(o_ve, 1)
                    pool.wait_ge(o_ve, b5 + 1)
                    g.tensor_tensor(rs_o[:, :], ve_o[:, :], minus_half[:, :], ALU.pow).then_inc(o_rs, 1)

            pipeline(pool, step, STEPS, LOOP0, B, RING)
            for q in range(RING):
                pool.wait_ge(scattered[q], ring4(B - RING + q, q, 32))
            pool.drain().then_inc(scatter_over, 1)
            pool.drain().then_inc(phase2_over, 1)
            pool.wait_ge(phase2_over, 5)

            def mix_step(s, q):
                b = s
                if isinstance(b, int) and b < MIXRING:
                    idx = rows_all[:, 2 * b:2 * b + 2]
                else:
                    pool.wait_ge(mix2, b - MIXRING + 1)
                    hold(1, b - MIXRING)
                    g.tensor_copy(g_idx[q][:, :], rows_all[:, bass.ds(b * 2, 2)]).then_inc(gi_done, 1)
                    pool.wait_ge(gi_done, b - MIXRING + 1)
                    hold(2, b - MIXRING)
                    idx = g_idx[q][:, :]
                for j, (y, done) in enumerate(((y1[q], y1_loaded[q]), (y2[q], y2_loaded[q]))):
                    g.indirect_dma_start(out=y[:, :], out_offset=None, in_=y_d,
                                         in_offset=bass.IndirectOffsetOnAxis(ap=idx[:, j:j + 1], axis=0)
                                         ).then_inc(done, 16)

            pipeline(pool, mix_step, B, 2 * MIXRING, B, MIXRING)

        @block.scalar
        def _(act):
            a = nc.scalar
            act.dma_start(gates_raw[:, 0:1], gx_d.rearrange("(a n) -> a n", a=1).to_broadcast([P, 1])).then_inc(const_dma, 16)
            act.dma_start(gates_raw[:, 1:2], gf_d.rearrange("(a n) -> a n", a=1).to_broadcast([P, 1])).then_inc(const_dma, 16)
            act.dma_start(wg1[:, :], wg1_d).then_inc(const_dma, 16)
            act.dma_start(wg2[:, :], wg2_d).then_inc(const_dma, 16)
            act.wait_ge(const_dma, 64)
            act.wait_ge(const_ready, 22)
            a.activation(gates[:, :], gates_raw[:, :], ACT.Tanh).then_inc(gate_ready, 1)
            act.wait_ge(gate_ready, 1)

            def step(s, u):
                b1, p1_, r1 = s - O_NORM, (u - O_NORM) % 2, (u - O_NORM) % RING
                b2, p2_ = s - O_QT, (u - O_QT) % 2
                b4 = s - O_ST
                b5 = s - O_OUT
                b6 = s - O_GATE
                for k in range(KV):
                    if valid(b4):
                        n = b4 * KV + k
                        act.wait_ge(st_done, n + 1)
                        if k == 0:
                            wait(act, pv_done, 2 * b4 - 1)
                        if k == 4:
                            wait(act, pv_done, 2 * b4)
                        a.activation(probs[:, k * G * S:(k + 1) * G * S], st_ps[k % 2][:, :], ACT.Exp,
                                     scale=HD ** -0.5).then_inc(exp_done, 1)
                    if k == 5 and valid(b1):
                        act.wait_ge(q_rem, b1 + 1)
                        a.activation(qn[:, :, 2, :], x_in[p1_][:, :].rearrange("p (h d) -> p h d", d=HD),
                                     ACT.Copy).then_inc(q_mid, 1)
                    if k not in TURN_DVE and valid(b2):
                        act.wait_ge(qt_done, b2 * KV + k + 1)
                        wait(act, st_done, (b2 - 2) * KV + k + 1)
                        a.activation(kq[p2_][0:QROWS, k * KQ:(k + 1) * KQ],
                                     qt_ps[k % 2][:, :].bitcast(BF16)[0:QROWS, 0:KQ], ACT.Copy).then_inc(qt_act, 1)
                    if k == 1 and valid(b5):
                        act.wait_ge(pv_done, 2 * b5 + 2)
                        act.wait_ge(on_done, 2 * b5 + 1)
                        a.activation(o_sb[:, :], bank_a[:, :], ACT.Copy).then_inc(o_copied, 1)
                    if k == 2 and valid(b6):
                        if isinstance(b6, int) and b6 == 0:
                            act.wait_ge(pads_done, 16)
                        act.wait_ge(zt_done, b6 + 1)
                        wait(act, lg1_done, b6)
                        a.activation(z_t[:, :], bank_b[:, :], ACT.Copy).then_inc(zt_copied, 1)
                    if k == 0 and valid(b1):
                        act.wait_ge(c_loaded[p1_], ring2(b1, p1_))
                        wait(act, qt_done, (b1 - 1) * KV)
                        kn = k_nat[p1_][:, :].rearrange("p (k j d) -> p k j d", j=PARTS, d=HD)
                        a.activation(kn[:, :, 2:5, :], c_in[p1_][:, :].rearrange("p (k d) -> p k d", d=HD)
                                     .unsqueeze(2).to_broadcast([P, KV, 3, HD]), ACT.Copy).then_inc(k_hi, 1)
                    if k == 3 and valid(b1):
                        act.wait_ge(n_done, b1 + 1)
                        wait(act, qt_done, (b1 - 1) * KV)
                        qn = q_nat[p1_][:, :].rearrange("p (h j d) -> p h j d", j=4, d=HD)
                        a.activation(qn[:, :, 0:2, :], x_in[p1_][:, :].rearrange("p (h d) -> p h d", d=HD)
                                     .unsqueeze(2).to_broadcast([P, H, 2, HD]), ACT.Copy).then_inc(q_hi, 1)
                    if k == 4 and valid(b6):
                        act.wait_ge(lg1_done, b6 + 1)
                        wait(act, lg2_done, b6)
                        a.activation(th_sb[:, :], bank_a[0:E, 0:S], ACT.Tanh).then_inc(th_done, 1)
                    if k == 5 and valid(b4):
                        act.wait_ge(pv_done, 2 * b4 + 1)
                        wait(act, on_done, 2 * b4)
                        a.activation(o_sb[:, :], bank_a[:, :], ACT.Copy).then_inc(o_copied, 1)
                    if k == 6 and valid(b1):
                        wait(act, pv_done, 2 * (b1 - 3))
                        a.activation(v_aug[r1][:, :].rearrange("p (k c) -> p k c", c=32)[:, :, 0:HD],
                                     c_in[p1_][:, :].rearrange("p (k d) -> p k d", d=HD), ACT.Copy,
                                     scale=gates[:, 0:1]).then_inc(v_done, 1)
                    if k == 7 and valid(s):
                        act.wait_ge(w_loaded, 16 * (s + 1))
                        a.activation(w_hi[:, bass.ds(s * WCHUNK, WCHUNK)], wst[:, :], ACT.Copy).then_inc(w_hi_done, 1)

            pipeline(act, step, STEPS, LOOP0, B, RING)
            act.wait_ge(gap_done, B)
            act.drain().then_inc(phase1_over, 1)
            act.wait_ge(phase1_over, 4)
            a.activation(egap[:, :], gap_all[:, :], ACT.Exp).then_inc(exp2_done, 1)

            def tile_step(s, u, fresh):
                t, p = s - 3, (u - 3) % 2
                if valid(t, TILES):
                    act.wait_ge(ht_done, t + 1)
                    wait(act, dn_done, t - 1)
                    a.activation(hh[p][:, :], bank[4 + p][:, 0:HE], ACT.Copy).then_inc(hh_done, 1)
                t, p = s - 1, (u - 1) % 2
                if valid(t, TILES):
                    act.wait_ge(ft_done, t + 1)
                    wait(act, up_done, t - 1)
                    a.activation(zh[p][:, :], bank[p][:, :], ACT.Copy).then_inc(zh_done, 1)
                t, p = s - 2, (u - 2) % 2
                if valid(t, TILES):
                    act.wait_ge(u_done, t + 1)
                    wait(act, h_done, t - 1)
                    a.activation(t_sb[p][:, :], u_sb[p][:, :], ACT.Tanh, scale=0.5).then_inc(tanh_done, 1)

            tile_pipeline(act, tile_step)
            act.drain().then_inc(phase2_over, 1)

        @block.vector
        def _(dve):
            v = nc.vector
            dve.wait_ge(const_ready, 22)

            def max_part(b, p, half, n):
                src = nmax[p][:, H // 2 * half:H // 2 * (half + 1)].rearrange("p (k g) -> p k g", g=G)
                hi, lo = (nm_parts[half][:, MHALF * j:MHALF * (j + 1)]
                          .rearrange("p (k c) -> p k c", c=G + 1)[:, :, 1:] for j in range(MROWS))
                cnt = 2 * b + half + 1
                if n == 0:
                    wait(dve, mt_done, cnt - 2)
                    dve.wait_ge(max_done, KV * b + 4 * half + 4)
                    v.tensor_copy(hi, src).then_inc(nm_hi, 1)
                if n == 1:
                    dve.wait_ge(nm_hi, cnt)
                    v.tensor_tensor(lo, src, hi, ALU.subtract).then_inc(nm_lo, 1)

            def max_copy(b, half, src):
                dve.wait_ge(mt_done, 2 * b + half + 1)
                wait(dve, mrow[half], 16 * b)
                v.tensor_copy(mt_sb[half][:, :], src[:, :].bitcast(BF16)[0:MROWS * MHALF, 0:S]).then_inc(mt_copied, 1)

            def weights_sum(b, grp):
                o = bank_b[:, :].rearrange("p (g k c) -> p g k c", g=G, c=32)
                dve.wait_ge(on_done, 2 * b + grp + 1)
                v.reciprocal(rden[:, :].rearrange("p (g k) -> p g k", g=G), o[:, :, :, HD]).then_inc(rden_done, 1)

            def attend(b, q, grp):
                o = bank_b[:, :].rearrange("p (g k c) -> p g k c", g=G, c=32)
                dve.wait_ge(rden_done, 2 * b + grp + 1)
                if grp == 0:
                    wait(dve, scattered[q], ring4(b - RING, q, 32))
                v.tensor_tensor(
                    z[q][:, :].rearrange("p (k g d) -> p g k d", g=G, d=HD)[:, :, 4 * grp:4 * grp + 4, :],
                    o[:, :, :, 0:HD],
                    rden[:, :].rearrange("p (g k) -> p g k", g=G).unsqueeze(3).to_broadcast([P, G, 4, HD]),
                    ALU.mult).then_inc(att_done, 1)

            def step(s, u):
                b0, p0_ = s - O_LOAD, (u - O_LOAD) % 2
                b1, p1_ = s - O_NORM, (u - O_NORM) % 2
                b2, p2_ = s - O_QT, (u - O_QT) % 2
                b3, p3_ = s - O_S, (u - O_S) % 2
                b4 = s - O_ST
                b5, p5_, q5 = s - O_OUT, (u - O_OUT) % 2, (u - O_OUT) % RING
                b6, p6_, q6 = s - O_GATE, (u - O_GATE) % 2, (u - O_GATE) % RING
                b7, p7_ = s - O_ROUTE, (u - O_ROUTE) % 2
                b8, p8_, q8 = s - O_SLOT, (u - O_SLOT) % 2, (u - O_SLOT) % RING
                for k in range(KV):
                    if valid(b3):
                        n = b3 * KV + k
                        dve.wait_ge(s_done, n + 1)
                        v.tensor_reduce(nmax[p3_][:, k * G:(k + 1) * G],
                                        s_ps[k % 2][:, :].rearrange("p (g t) -> p g t", g=G),
                                        X_AXIS, ALU.max, negate=True).then_inc(max_done, 1)
                    if k in TURN_DVE and valid(b2):
                        dve.wait_ge(qt_done, b2 * KV + k + 1)
                        wait(dve, st_done, (b2 - 2) * KV + k + 1)
                        v.tensor_copy(kq[p2_][0:QROWS, k * KQ:(k + 1) * KQ],
                                      qt_ps[k % 2][:, :].bitcast(BF16)[0:QROWS, 0:KQ]).then_inc(qt_dve, 1)
                    if k == 0:
                        if valid(b7):
                            dve.wait_ge(lg_copied, b7 + 1)
                        if valid(b4):
                            max_copy(b4, 1, bank_a)
                        if valid(b6):
                            dve.wait_ge(o_rs, b6 + 1)
                            v.tensor_scalar(z[q6][:, :], x_res[p6_][:, :], mv_o[:, 0:1], rs_o[:, :], ALU.subtract,
                                            ALU.mult).then_inc(z_done, 1)
                        if valid(b7):
                            v.max(top8[:, :], lg_sb[p7_][:, :]).then_inc(top_done, 1)
                        if valid(b8):
                            dve.wait_ge(pos_done, b8 + 1)
                            v.tensor_tensor_reduce(out=junk[:, 0:E], in0=m1[p8_][:, :], in1=pos[:, :], scale=1.0,
                                                   scalar=0.0, op0=ALU.mult, op1=ALU.add,
                                                   accum_out=slot_f[:, 0:1]).then_inc(slot_done, 1)
                            v.tensor_tensor_reduce(out=junk[:, E:2 * E], in0=m2[p8_][:, :], in1=pos[:, :], scale=1.0,
                                                   scalar=0.0, op0=ALU.mult, op1=ALU.add,
                                                   accum_out=slot_f[:, 1:2]).then_inc(slot_done, 1)
                    if k == 1:
                        if valid(b5):
                            weights_sum(b5, 0)
                        if valid(b8):
                            dve.wait_ge(slot_done, 2 * b8 + 2)
                            v.tensor_copy(slot_i[q8][:, :], slot_f[:, :]).then_inc(sloti_done, 1)
                            v.tensor_copy(slot_all[:, bass.ds(b8 * 2, 2)], slot_f[:, :]).then_inc(slotall_done, 1)
                        if valid(b5):
                            attend(b5, q5, 0)
                        if valid(b7):
                            dve.wait_ge(top_done, b7 + 1)
                            v.tensor_tensor(gap_all[:, bass.ds(b7, 1)], top8[:, 1:2], top8[:, 0:1],
                                            ALU.subtract).then_inc(gap_done, 1)
                            v.max_index(idx8[:, :], top8[:, :], lg_sb[p7_][:, :]).then_inc(idx_done, 1)
                    if k == 2:
                        if valid(b1):
                            dve.wait_ge(n_rs, b1 + 1)
                            v.tensor_scalar(x_in[p1_][:, :], x_in[p1_][:, :], mv_n[:, 0:1], rs_n[:, :], ALU.subtract,
                                            ALU.mult).then_inc(n_done, 1)
                        if valid(b7):
                            dve.wait_ge(idx_done, b7 + 1)
                            v.tensor_copy(idxf[:, :], idx8[:, 0:2]).then_inc(idxf_done, 1)
                    if k == 3:
                        if valid(b7):
                            dve.wait_ge(idxf_done, b7 + 1)
                            v.tensor_scalar(m1[p7_][:, :], e_diff[:, 0:E], idxf[:, 0:1], None,
                                            ALU.is_equal).then_inc(masks_done, 1)
                        if valid(b3):
                            max_part(b3, p3_, 0, 0)
                        if valid(b7):
                            v.tensor_scalar(m2[p7_][:, :], e_diff[:, 0:E], idxf[:, 1:2], None,
                                            ALU.is_equal).then_inc(masks_done, 1)
                        if valid(b3):
                            max_part(b3, p3_, 0, 1)
                    if k == 4:
                        if valid(b5):
                            weights_sum(b5, 1)
                        if valid(b7):
                            dve.wait_ge(masks_done, 2 * b7 + 2)
                            v.tensor_tensor(m12[p7_][:, :], m1[p7_][:, :], m2[p7_][:, :], ALU.add).then_inc(m12_done, 1)
                        if valid(b5):
                            attend(b5, q5, 1)
                    if k == 5:
                        if valid(b0):
                            dve.wait_ge(x_loaded[p0_], ring2(b0, p0_))
                            v.bn_stats(st_n[:, :], x_in[p0_][:, :]).then_inc(n_stats, 1)
                        if valid(b3):
                            max_copy(b3, 0, bank_b)
                    if k == 6:
                        if valid(b0):
                            dve.wait_ge(n_stats, b0 + 1)
                        if valid(b5):
                            dve.wait_ge(res_done, b5 + 1)
                            v.bn_stats(st_o[:, :], x_res[p5_][:, :]).then_inc(o_stats, 1)
                        if valid(b0):
                            v.bn_aggr(mv_n[:, :], st_n[:, :]).then_inc(n_mv, 1)
                    if k == 7:
                        if valid(b5):
                            dve.wait_ge(o_stats, b5 + 1)
                        if valid(b7):
                            dve.wait_ge(rank_done, b7 + 1)
                            wait(dve, run_done, b7)
                            v.tensor_tensor(pos[:, :], bank_b[:, 0:E], run[:, :], ALU.add).then_inc(pos_done, 1)
                            v.tensor_tensor(run[:, :], run[:, :], bank_b[:, E:2 * E], ALU.add).then_inc(run_done, 1)
                        if valid(b3):
                            max_part(b3, p3_, 1, 0)
                        if valid(b5):
                            v.bn_aggr(mv_o[:, :], st_o[:, :]).then_inc(o_mv, 1)
                        if valid(b3):
                            max_part(b3, p3_, 1, 1)
                        if valid(b6):
                            dve.wait_ge(lg2_done, b6 + 1)
                            v.tensor_copy(lg_sb[p6_][:, :], bank_a[:, 0:E]).then_inc(lg_copied, 1)

            pipeline(dve, step, STEPS, LOOP0, B, RING)
            dve.wait_ge(run_done, B)
            dve.wait_ge(w_lo_done, B)
            dve.drain().then_inc(phase1_over, 1)
            dve.wait_ge(phase1_over, 4)

            link = [0]

            def step_of(ins):
                link[0] += 1
                ins.then_inc(tab_step, 1)

            def then(ins):
                step_of(ins)
                dve.wait_ge(tab_step, link[0])

            then(v.tensor_tensor(count[:, :], run[:, :], ebase[:, :], ALU.subtract))
            ov = past[:, 0:E * B].rearrange("p (e i) -> p e i", e=E)
            step_of(v.tensor_scalar(upto[:, :], e_diff[:, :], 0.0, None, ALU.is_le))
            then(v.scalar_tensor_tensor(ov, count[:, :].unsqueeze(2).to_broadcast([P, E, B]), 1.0 / P,
                                        iota_t[:, 0:B].unsqueeze(1).to_broadcast([P, E, B]), ALU.mult, ALU.is_gt))
            then(v.tensor_reduce(ntile[:, :], ov, X_AXIS, ALU.add))
            un = upton[:, :].rearrange("p (e i) -> p e i", e=E)
            step_of(v.memset(drop[:, E:E + 1], 0.0))
            then(v.tensor_tensor(un, upto[:, :].rearrange("p (e i) -> p e i", e=E),
                                 ntile[:, :].unsqueeze(1).to_broadcast([P, E, E]), ALU.mult))
            then(v.tensor_reduce(tend[:, :], un, X_AXIS, ALU.add))
            then(v.scalar_tensor_tensor(row0[:, :], tend[:, :], float(-P), run[:, :], ALU.mult, ALU.add))
            step_of(v.tensor_copy(drop[:, 0:1], row0[:, 0:1]))
            step_of(v.tensor_tensor(drop[:, 1:E], row0[:, 1:E], row0[:, 0:E - 1], ALU.subtract))
            pv_ = past[:, :].rearrange("p (t e) -> p t e", e=E)
            pw_ = pastw[:, :].rearrange("p (t e) -> p t e", e=E)
            then(v.tensor_tensor(pv_, iota_t[:, :].unsqueeze(2).to_broadcast([P, TILES, E]),
                                 tend[:, :].unsqueeze(1).to_broadcast([P, TILES, E]), ALU.is_ge))
            step_of(v.tensor_tensor(pw_, pv_, drop[:, 1:E + 1].unsqueeze(1).to_broadcast([P, TILES, E]), ALU.mult))
            then(v.tensor_reduce(tile_e[:, :], pv_, X_AXIS, ALU.add))
            step_of(v.tensor_scalar(live[:, :], tile_e[:, :], float(E), None, ALU.is_lt))
            then(v.tensor_reduce(tile_r[:, :], pw_, X_AXIS, ALU.add))
            then(v.scalar_tensor_tensor(row_f[:, :], iota_t[:, :], float(P), tile_r[:, :], ALU.mult, ALU.add))
            v.scalar_tensor_tensor(tab_r[:, :], row_f[:, :], row0[:, 0:1], live[:, :], ALU.add,
                                   ALU.mult).then_inc(tab_done, 1)
            v.tensor_scalar(tab_e[:, :], tile_e[:, :], float(E - 1), None, ALU.min).then_inc(tab_done, 1)
            bv = pastw[:, 0:2 * B * E].rearrange("p (n e) -> p n e", e=E)
            then(v.tensor_tensor(bv, slot_all[:, :].unsqueeze(2).to_broadcast([P, 2 * B, E]),
                                 ebase[:, :].unsqueeze(1).to_broadcast([P, 2 * B, E]), ALU.is_ge))
            then(v.tensor_tensor(bv, bv, drop[:, 0:E].unsqueeze(1).to_broadcast([P, 2 * B, E]), ALU.mult))
            then(v.tensor_reduce(shift[:, :], bv, X_AXIS, ALU.add))
            then(v.tensor_tensor(rows_all[:, :], slot_all[:, :], shift[:, :], ALU.subtract))
            dve.wait_ge(exp2_done, 1)
            then(v.tensor_scalar(sden[:, :], egap[:, :], 1.0, None, ALU.add))
            then(v.reciprocal(sden[:, :], sden[:, :]))
            dve.wait_ge(gate_ready, 1)
            then(v.tensor_scalar(coef[0][:, :], sden[:, :], gates[:, 1:2], None, ALU.mult))
            v.tensor_tensor(coef[1][:, :], coef[0][:, :], egap[:, :], ALU.mult).then_inc(coef_step, 1)
            dve.wait_ge(tab_done, 2)

            expert = [None, None]

            def tile_step(s, u, fresh):
                expert[1] = expert[0]
                if valid(s - 2, TILES):
                    expert[0] = expert_of(dve, s - 2)
                t, p = s - 3, (u - 3) % 2
                if valid(t, TILES):
                    dve.wait_ge(hh_done, t + 1)
                    wait(dve, dn_done, t - 1)
                    v.tensor_tensor(hl[p][:, :], bank[4 + p][:, 0:HE], hh[p][:, :].bitcast(F32),
                                    ALU.subtract).then_inc(hl_done, 1)
                t, p = s - 1, (u - 1) % 2
                if valid(t, TILES):
                    dve.wait_ge(zh_done, t + 1)
                    wait(dve, up_done, t - 1)
                    v.tensor_tensor(zl[p][:, :], bank[p][:, :], zh[p][:, :].bitcast(F32),
                                    ALU.subtract).then_inc(zl_done, 1)
                t, p = s - 2, (u - 2) % 2
                if valid(t, TILES):
                    e = expert[0]
                    if isinstance(t, int) and t == 0:
                        dve.wait_ge(bup_loaded, 16)
                    dve.wait_ge(up_done, t + 1)
                    wait(dve, tanh_done, t - 1)
                    v.tensor_tensor(u_sb[p][:, :], bank[2 + p][:, 0:HE], bup[:, bass.ds(e * HE, HE)],
                                    ALU.add).then_inc(u_done, 1)
                    dve.wait_ge(tanh_done, t + 1)
                    wait(dve, ht_done, t - 1)
                    v.scalar_tensor_tensor(h_sb[p][:, :], t_sb[p][:, :], 1.0, u_sb[p][:, :], ALU.add,
                                           ALU.mult).then_inc(h_done, 1)
                t, p = s - 3, (u - 3) % 2
                if valid(t, TILES):
                    e = expert_of(dve, t) if fresh else expert[1]
                    if isinstance(t, int) and t == 0:
                        dve.wait_ge(bdn_loaded, 16)
                    dve.wait_ge(dn_done, t + 1)
                    wait(dve, y_stored[p], ring2(t - 2, p))
                    v.scalar_tensor_tensor(y_sb[p][:, :], bank[6 + p][:, :], 0.5, bdn[:, bass.ds(e * D, D)],
                                           ALU.mult, ALU.add).then_inc(y_done, 1)

            tile_pipeline(dve, tile_step)
            dve.drain().then_inc(phase2_over, 1)

            def mix_step(s, q):
                b = s
                dve.wait_ge(r_loaded[q], mixed(b, q))
                dve.wait_ge(y1_loaded[q], mixed(b, q))
                v.scalar_tensor_tensor(residual(b), y1[q][:, :], coef[0][:, bass.ds(b, 1)], residual(b),
                                       ALU.mult, ALU.add).then_inc(mix1, 1)
                dve.wait_ge(mix1, b + 1)
                dve.wait_ge(y2_loaded[q], mixed(b, q))
                v.scalar_tensor_tensor(residual(b), y2[q][:, :], coef[1][:, bass.ds(b, 1)], residual(b),
                                       ALU.mult, ALU.add).then_inc(mix2, 1)

            pipeline(dve, mix_step, B, MIXRING, B, MIXRING)

        @block.tensor
        def _(pe):
            t_ = nc.tensor
            pe.wait_ge(const_ready, 22)
            pe.wait_ge(const_dma, 64)

            def step(s, u):
                b2, p2_ = s - O_QT, (u - O_QT) % 2
                b3, p3_ = s - O_S, (u - O_S) % 2
                b4, p4_, r4 = s - O_ST, (u - O_ST) % 2, (u - O_ST) % RING
                b5, r5 = s - O_OUT, (u - O_OUT) % RING
                b6, q6 = s - O_GATE, (u - O_GATE) % RING
                b7, p7_ = s - O_ROUTE, (u - O_ROUTE) % 2
                b8 = s - O_SLOT

                def weighted_sum(b, r, grp):
                    for j in range(4):
                        k = 4 * grp + j
                        last = t_.matmul(bank_a[32 * j:32 * j + 32, :], v_aug[r][:, 32 * k:32 * k + 32],
                                         probs[:, k * G * S:(k + 1) * G * S], start=True, stop=True,
                                         tile_position=(0, 32 * j))
                    last.then_inc(pv_done, 1)

                def rows_back(b, grp):
                    pe.wait_ge(o_copied, 2 * b + grp + 1)
                    for g_ in range(G):
                        last = t_.transpose(bank_b[:, P * g_:P * g_ + P], o_sb[:, S * g_:S * g_ + S], ident_f[:, :])
                    last.then_inc(on_done, 1)

                def turn_maxima(b, half, dst):
                    pe.wait_ge(nm_lo, 2 * b + half + 1)
                    t_.transpose(dst[:, :].bitcast(BF16)[0:MWIDE, 0:S], nm_parts[half][:, :],
                                 ident_b[:, :]).then_inc(mt_done, 1)

                for k in range(KV):
                    if valid(b2):
                        if k == 0:
                            pe.wait_ge(q_lo, b2 + 1)
                            pe.wait_ge(k_lo, b2 + 1)
                        on_dve, count = turned(k - 2, b2) if k >= 2 else turned(k - 2 + KV, b2 - 1)
                        wait(pe, qt_dve if on_dve else qt_act, count)
                        dst = qt_ps[k % 2][:, :].bitcast(BF16)
                        t_.transpose(dst[0:QROWS, 0:P], k_nat[p2_][:, k * QROWS:(k + 1) * QROWS], ident_b[:, :])
                        for g_ in range(G):
                            h = k * G + g_
                            c0, cols = h * 4 * HD, slice(P + P * g_, 2 * P + P * g_)
                            t_.transpose(dst[0:4 * HD, cols], q_nat[p2_][:, c0:c0 + 4 * HD], ident_b[:, :])
                            last = t_.transpose(dst[4 * HD:QROWS, cols], q_nat[p2_][:, c0 + HD:c0 + 3 * HD],
                                                ident_b[:, :], tile_position=(0, 4 * HD))
                        last.then_inc(qt_done, 1)
                    if valid(b3):
                        on_dve, count = turned(k, b3)
                        pe.wait_ge(qt_dve if on_dve else qt_act, count)
                        wait(pe, max_done, b3 * KV + (k - 1))
                        c = k * KQ
                        for g_ in range(G):
                            last = t_.matmul(s_ps[k % 2][:, P * g_:P * g_ + P],
                                             kq[p3_][0:QROWS, c + P + P * g_:c + 2 * P + P * g_],
                                             kq[p3_][0:QROWS, c:c + P], start=True, stop=True)
                        last.then_inc(s_done, 1)
                    if valid(b4):
                        if k % 4 == 0:
                            pe.wait_ge(mrow[k // 4], 16 * (b4 + 1))
                        wait(pe, exp_done, b4 * KV + (k - 1))
                        c = k * KQ
                        t_.matmul(st_ps[k % 2][:, :], kq[p4_][0:QROWS + MROWS, c:c + P],
                                  kq[p4_][0:QROWS + MROWS, c + P:c + KQ], start=True, stop=True).then_inc(st_done, 1)
                    if k == 0:
                        if valid(b5):
                            if valid(b8):
                                pe.wait_ge(run_done, b8 + 1)
                            elif valid(b4):
                                pe.wait_ge(mt_copied, 2 * b4 + 1)
                            rows_back(b5, 0)
                        if valid(b4):
                            if valid(b7):
                                pe.wait_ge(lg_copied, b7 + 1)
                            elif valid(b5):
                                pe.wait_ge(o_copied, 2 * b5 + 1)
                            turn_maxima(b4, 1, bank_a)
                    if k == 1 and valid(b5):
                        pe.wait_ge(exp_done, KV * b5 + KV)
                        if valid(b4):
                            pe.wait_ge(mt_copied, 2 * b4 + 2)
                        else:
                            pe.wait_ge(lg_copied, b7 + 1)
                        weighted_sum(b5, r5, 1)
                    if k == 2 and valid(b6):
                        pe.wait_ge(z_done, b6 + 1)
                        if valid(b5):
                            pe.wait_ge(att_done, 2 * b5 + 1)
                        else:
                            pe.wait_ge(run_done, b8 + 1)
                        for c in range(DC):
                            last = t_.transpose(bank_b[:, P * c:P * c + P], z[q6][:, P * c:P * c + P], ident_f[:, :])
                        last.then_inc(zt_done, 1)
                    if k == 3 and valid(b5):
                        if valid(b6):
                            pe.wait_ge(zt_copied, b6 + 1)
                        else:
                            pe.wait_ge(att_done, 2 * b5 + 1)
                        rows_back(b5, 1)
                    if k == 4 and valid(b6):
                        pe.wait_ge(zt_copied, b6 + 1)
                        if valid(b5):
                            pe.wait_ge(o_copied, 2 * b5 + 2)
                        else:
                            pe.wait_ge(lg_copied, b7 + 1)
                        for c in range(DC):
                            last = t_.matmul(bank_a[0:E, 0:S], wg1[:, c * E:(c + 1) * E], z_t[:, P * c:P * c + P],
                                             start=(c == 0), stop=(c == DC - 1))
                        last.then_inc(lg1_done, 1)
                    if k == 5 and valid(b4):
                        pe.wait_ge(exp_done, KV * b4 + 4)
                        pe.wait_ge(v_done, b4 + 1)
                        if valid(b6):
                            pe.wait_ge(th_done, b6 + 1)
                        elif valid(b5):
                            pe.wait_ge(o_copied, 2 * b5 + 2)
                        else:
                            pe.wait_ge(mt_copied, 2 * b4 + 2)
                        weighted_sum(b4, r4, 0)
                    if k == 5 and valid(b3):
                        if valid(b5):
                            pe.wait_ge(att_done, 2 * b5 + 2)
                        elif valid(b4):
                            wait(pe, mt_copied, 2 * b4 + 1)
                        turn_maxima(b3, 0, bank_b)
                    if k == 6:
                        if valid(b7):
                            pe.wait_ge(m12_done, b7 + 1)
                            if valid(b3):
                                pe.wait_ge(mt_copied, 2 * b3 + 1)
                            elif valid(b5):
                                pe.wait_ge(att_done, 2 * b5 + 2)
                            elif valid(b6):
                                pe.wait_ge(zt_copied, b6 + 1)
                            else:
                                pe.wait_ge(run_done, b7)
                            t_.matmul(bank_b[:, 0:E], before[:, :], m12[p7_][:, :], start=True, stop=True)
                            t_.matmul(bank_b[:, E:2 * E], ones_b[:, :], m12[p7_][:, :], start=True,
                                      stop=True).then_inc(rank_done, 1)
                    if k == 7:
                        if valid(b6):
                            pe.wait_ge(th_done, b6 + 1)
                            if valid(b4):
                                pe.wait_ge(o_copied, 2 * b4 + 1)
                            t_.matmul(bank_a[:, 0:E], th_sb[:, :], wg2[:, :], start=True, stop=True).then_inc(lg2_done, 1)

            pipeline(pe, step, STEPS, LOOP0, B, RING)
            pe.drain().then_inc(phase1_over, 1)
            pe.wait_ge(phase1_over, 4)
            pe.wait_ge(tab_done, 2)

            expert = [None, None]

            def tile_step(s, u, fresh):
                expert[1] = expert[0]
                if valid(s - 2, TILES):
                    expert[0] = expert_of(pe, s - 2)
                t, p, r = s - 1, (u - 1) % 2, (u - 1) % RING
                if valid(t, TILES):
                    pe.wait_ge(tile_loaded[r], ring4(t, r, 16))
                    for c in range(DC):
                        last = t_.transpose(bank[p][:, P * c:P * c + P], z_s[r][:, P * c:P * c + P], ident_f[:, :])
                    last.then_inc(ft_done, 1)
                t, p = s - 3, (u - 3) % 2
                if valid(t, TILES):
                    pe.wait_ge(h_done, t + 1)
                    for c in range(HC):
                        last = t_.transpose(bank[4 + p][:, P * c:P * c + P], h_sb[p][:, P * c:P * c + P], ident_f[:, :])
                    last.then_inc(ht_done, 1)
                t, p = s - 2, (u - 2) % 2
                if valid(t, TILES):
                    pe.wait_ge(zl_done, t + 1)
                    o = bank[2 + p][:, 0:HE]
                    for c in range(DC):
                        cols = bass.ds(expert[0] * (DC * HE) + c * HE, HE)
                        t_.matmul(o, zh[p][:, P * c:P * c + P], w_hi[:, cols], start=(c == 0), stop=False)
                        t_.matmul(o, zh[p][:, P * c:P * c + P], w_lo[:, cols], start=False, stop=False)
                        last = t_.matmul(o, zl[p][:, P * c:P * c + P], w_hi[:, cols], start=False, stop=(c == DC - 1))
                    last.then_inc(up_done, 1)
                t, p = s - 3, (u - 3) % 2
                if valid(t, TILES):
                    if fresh:
                        expert[1] = expert_of(pe, t)
                    wait(pe, y_done, t - 1)
                    pe.wait_ge(hl_done, t + 1)
                    for c in range(HC):
                        cols = bass.ds(expert[1] * (HC * D) + (DOWN0 + c * D), D)
                        o = bank[6 + p][:, :]
                        t_.matmul(o, hh[p][:, P * c:P * c + P], w_hi[:, cols], start=(c == 0), stop=False)
                        t_.matmul(o, hh[p][:, P * c:P * c + P], w_lo[:, cols], start=False, stop=False)
                        last = t_.matmul(o, hl[p][:, P * c:P * c + P], w_hi[:, cols], start=False, stop=(c == HC - 1))
                    last.then_inc(dn_done, 1)

            tile_pipeline(pe, tile_step)
            pe.drain().then_inc(phase2_over, 1)


_INS = ["x", "ctx_512", "g_xattn", "g_ffn", "wg1", "wg2", "w", "bup", "bdn"]


def kernel(x, ctx_512, g_xattn, g_ffn, L0_ffn_Wg1, L0_ffn_Wg2, L0_ffn_Wup, L0_ffn_bup, L0_ffn_Wdown, L0_ffn_bdown):
    import numpy as np
    import concourse.bacc as bacc
    from concourse.bass_utils import run_bass_kernel_spmd

    wup, wdown = np.asarray(L0_ffn_Wup), np.asarray(L0_ffn_Wdown)
    up = wup.reshape(E, HE, DC, P).transpose(3, 0, 2, 1).reshape(P, DOWN0)
    down = wdown.reshape(E, D, HC, P).transpose(3, 0, 2, 1).reshape(P, WCOLS - DOWN0)
    w = np.concatenate([up, down], axis=1).reshape(P, WCOLS // WCHUNK, WCHUNK).transpose(1, 0, 2)
    data = {
        "x": x, "ctx_512": ctx_512, "g_xattn": g_xattn, "g_ffn": g_ffn,
        "wg1": np.asarray(L0_ffn_Wg1).reshape(E, DC, P).transpose(2, 1, 0).reshape(P, DC * E),
        "wg2": np.asarray(L0_ffn_Wg2).T,
        "w": w,
        "bup": np.asarray(L0_ffn_bup).reshape(1, E * HE),
        "bdn": np.asarray(L0_ffn_bdown).reshape(1, E * D),
    }
    nc = bacc.Bacc("TRN2", target_bir_lowering=False, num_devices=1)
    arrays, args = {}, []
    for name in _INS:
        a = np.ascontiguousarray(data[name])
        arrays[f"in_{name}"] = a
        args.append(nc.dram_tensor(f"in_{name}", a.shape, mybir.dt.from_np(a.dtype), kind="ExternalInput").ap())
    out = nc.dram_tensor("out", (B, S, D), F32, kind="ExternalOutput").ap()
    block_kernel(nc, *args, out)
    r = run_bass_kernel_spmd(nc, [arrays], core_ids=[0])
    return r.results[0]["out"]
```
